# Optimizing a Trainium2 kernel written in Bass

```python
import numpy as np
import jax
import jax.numpy as jnp

def _softmax(x, axis=-1):
    return jax.nn.softmax(x, axis=axis)

def _gelu(x):
    return jax.nn.gelu(x, approximate=True)

def _silu(x):
    return jax.nn.silu(x)

def _sigmoid(x):
    return jax.nn.sigmoid(x)

def _layernorm(x, axis=-1, eps=1e-05):
    m = jnp.mean(x, axis=axis, keepdims=True)
    v = jnp.var(x, axis=axis, keepdims=True)
    return (x - m) / jnp.sqrt(v + eps)

def _scatter_add(tgt, idx, src, axis=0):
    return tgt.at[idx].add(src)

def _segment_sum(src, seg, n):
    return jax.ops.segment_sum(src, seg, n)
kernel_name = 'mk_gnn_resnorm_d2_gnn_r64_39d3de'

def setup_inputs(seed: int=0):
    np.random.seed(seed)
    _w = jnp.asarray

    def _rec_inputs():
        import jax
        import jax.numpy as jnp
        _gk = jax.random.key(seed)
        x = -0.0003713 + 1 * jax.random.normal(jax.random.fold_in(_gk, 1), (50000, 128), jnp.float32)
        src = jax.random.randint(jax.random.fold_in(_gk, 2), (12500,), 0, 50000, jnp.int32)
        dst = jnp.minimum((50000 * jax.random.uniform(jax.random.fold_in(_gk, 3), (12500,)) ** 2.0).astype(jnp.int32), 49999)
        _o = jnp.argsort(dst, stable=True)
        src = src[_o]
        dst = dst[_o]
        edge_attr_128 = -5.16925e-05 + 1.00005 * jax.random.normal(jax.random.fold_in(_gk, 11), (12500, 128), jnp.float32)
        return (x, src, dst, edge_attr_128)
    x, src, dst, edge_attr_128 = _rec_inputs()

    def _L0_gnn_setup():
        import jax, jax.numpy as jnp
        import numpy as np
        N = 100000
        E = 25000
        IN_DIM = 128
        HID = 128
        OUT = 128

        def _agg_mean(feat, row, col, inv_deg, n):
            summed = jax.ops.segment_sum(feat[col], row, num_segments=n)
            return summed * inv_deg[:, None]
        key = jax.random.key(seed)
        ks = jax.random.split(key, 8)
        x = jax.random.normal(ks[0], (N, IN_DIM), dtype=jnp.float32)
        edge_index = jax.random.randint(ks[1], (2, E), 0, N, dtype=jnp.int32)
        s1 = 1.0 / np.sqrt(IN_DIM)
        s2 = 1.0 / np.sqrt(HID)
        s3 = 1.0 / np.sqrt(2 * HID)
        W1 = jax.random.uniform(ks[2], (IN_DIM, HID), jnp.float32, -s1, s1)
        b1 = jax.random.uniform(ks[3], (HID,), jnp.float32, -s1, s1)
        W2 = jax.random.uniform(ks[4], (HID, HID), jnp.float32, -s2, s2)
        b2 = jax.random.uniform(ks[5], (HID,), jnp.float32, -s2, s2)
        Wout = jax.random.uniform(ks[6], (2 * HID, OUT), jnp.float32, -s3, s3)
        bout = jax.random.uniform(ks[7], (OUT,), jnp.float32, -s3, s3)
        return {'x': x, 'edge_index': edge_index, 'W1': W1, 'b1': b1, 'W2': W2, 'b2': b2, 'Wout': Wout, 'bout': bout}
    _L0_gnn_all = _L0_gnn_setup()
    _L0_gnn_in = {k: v for k, v in _L0_gnn_all.items() if k in ('W1', 'b1', 'W2', 'b2', 'Wout', 'bout')}
    del _L0_gnn_all

    def _L1_gnn_setup():
        import jax, jax.numpy as jnp
        import numpy as np
        N_NODES = 50000
        N_EDGES = 12500
        D = 128
        key = jax.random.key(seed)
        ks = jax.random.split(key, 7)
        x = jax.random.normal(ks[0], (N_NODES, D), dtype=jnp.float32)
        edge_index = jax.random.randint(ks[1], (2, N_EDGES), 0, N_NODES, dtype=jnp.int32)
        edge_attr = jax.random.normal(ks[2], (N_EDGES, D), dtype=jnp.float32)
        W1 = jax.random.normal(ks[3], (D, D), dtype=jnp.float32) / np.sqrt(D)
        b1 = jnp.zeros((D,), dtype=jnp.float32)
        W2 = jax.random.normal(ks[4], (D, D), dtype=jnp.float32) / np.sqrt(D)
        b2 = jnp.zeros((D,), dtype=jnp.float32)
        eps = jnp.zeros((), dtype=jnp.float32)
        return {'x': x, 'edge_index': edge_index, 'edge_attr': edge_attr, 'W1': W1, 'b1': b1, 'W2': W2, 'b2': b2, 'eps': eps}
    _L1_gnn_all = _L1_gnn_setup()
    _L1_gnn_in = {k: v for k, v in _L1_gnn_all.items() if k in ('W1', 'b1', 'W2', 'b2', 'eps')}
    del _L1_gnn_all
    return {'x': x, 'src': src, 'dst': dst, 'edge_attr_128': edge_attr_128, 'L0_gnn_W1': _L0_gnn_in['W1'], 'L0_gnn_b1': _L0_gnn_in['b1'], 'L0_gnn_W2': _L0_gnn_in['W2'], 'L0_gnn_b2': _L0_gnn_in['b2'], 'L0_gnn_Wout': _L0_gnn_in['Wout'], 'L0_gnn_bout': _L0_gnn_in['bout'], 'L1_gnn_W1': _L1_gnn_in['W1'], 'L1_gnn_b1': _L1_gnn_in['b1'], 'L1_gnn_W2': _L1_gnn_in['W2'], 'L1_gnn_b2': _L1_gnn_in['b2'], 'L1_gnn_eps': _L1_gnn_in['eps']}

def reference(x, src, dst, edge_attr_128, L0_gnn_W1, L0_gnn_b1, L0_gnn_W2, L0_gnn_b2, L0_gnn_Wout, L0_gnn_bout, L1_gnn_W1, L1_gnn_b1, L1_gnn_W2, L1_gnn_b2, L1_gnn_eps):
    import jax
    import jax.numpy as jnp

    def _L0_gnn_ref(x, edge_index, W1, b1, W2, b2, Wout, bout):
        import jax, jax.numpy as jnp
        import numpy as np
        N = 100000
        E = 25000
        IN_DIM = 128
        HID = 128
        OUT = 128

        def _agg_mean(feat, row, col, inv_deg, n):
            summed = jax.ops.segment_sum(feat[col], row, num_segments=n)
            return summed * inv_deg[:, None]
        n = x.shape[0]
        self_idx = jnp.arange(n, dtype=edge_index.dtype)
        row = jnp.concatenate([edge_index[0], self_idx])
        col = jnp.concatenate([edge_index[1], self_idx])
        deg = jax.ops.segment_sum(jnp.ones_like(row, dtype=x.dtype), row, num_segments=n)
        inv_deg = 1.0 / jnp.maximum(deg, 1.0)
        x1 = _agg_mean(x, row, col, inv_deg, n)
        x1 = jax.nn.relu(x1 @ W1 + b1)
        x2 = _agg_mean(x1, row, col, inv_deg, n)
        x2 = jax.nn.relu(x2 @ W2 + b2)
        h = jnp.concatenate([x1, x2], axis=-1)
        node_repr = h @ Wout + bout
        return node_repr

    def _L1_gnn_ref(x, edge_index, edge_attr, W1, b1, W2, b2, eps):
        import jax, jax.numpy as jnp
        import numpy as np
        N_NODES = 50000
        N_EDGES = 12500
        D = 128
        src = edge_index[0]
        dst = edge_index[1]
        msg = jax.nn.relu(x[src] + edge_attr)
        agg = jax.ops.segment_sum(msg, dst, num_segments=x.shape[0])
        h = (1.0 + eps) * x + agg
        h = jax.nn.relu(h @ W1 + b1)
        return h @ W2 + b2
    edge_index = jnp.stack([src, dst])
    x = _layernorm(x + _L0_gnn_ref(x, edge_index, L0_gnn_W1, L0_gnn_b1, L0_gnn_W2, L0_gnn_b2, L0_gnn_Wout, L0_gnn_bout), axis=-1)
    x = _layernorm(x + _L1_gnn_ref(x, edge_index, edge_attr_128, L1_gnn_W1, L1_gnn_b1, L1_gnn_W2, L1_gnn_b2, L1_gnn_eps), axis=-1)
    return x

_drawn_inputs = setup_inputs


def setup_inputs(seed=0):
    import zlib

    import numpy as np

    out = dict(_drawn_inputs(seed))
    spreads = {'L1_gnn_b1': (0.0, 0.1), 'L1_gnn_b2': (0.0, 0.1)}
    factors = {'L0_gnn_b1': 3.725, 'L0_gnn_b2': 3.649}
    for name, (base, spread) in spreads.items():
        noise = np.random.default_rng([zlib.crc32(name.encode()), seed]).standard_normal(out[name].shape)
        drawn = base * np.exp(spread * noise) if base else spread * noise
        out[name] = jnp.asarray(drawn.astype(out[name].dtype))
    for name, factor in factors.items():
        out[name] = (out[name] * factor).astype(out[name].dtype)
    return out
```

```python
import concourse.bass as bass
from concourse import mybir
from contextlib import ExitStack

F32 = mybir.dt.float32
I32 = mybir.dt.int32
ALU = mybir.AluOpType
ACT = mybir.ActivationFunctionType

R = 7
RD = 6


class At:

    def __init__(self, ring, i, off):
        self.ring, self.i, self.off = ring, i, off
        self.k = ring * i + off
        self.slot = off % ring
        self.lap = i + off // ring

    def at(self, d):
        return At(self.ring, self.i, self.off + d)

    def is_any(self, *ks):
        return isinstance(self.k, int) and self.k in ks

    def is_from(self, k):
        return isinstance(self.k, int) and self.k >= k


def edge(k):
    return At(R, 0, k)


def dense(k):
    return At(RD, 0, k)


def steps(eng, body, ring, count):
    laps = (count - 2 * ring) // ring
    for k in range(ring):
        body(At(ring, 0, k))
    with eng.Fori(0, laps) as i:
        for u in range(ring):
            body(At(ring, i, ring + u))
    for k in range(ring * (laps + 1), count):
        body(At(ring, 0, k))


def wait(eng, sem, value):
    if not (isinstance(value, int) and value == 0):
        eng.wait_ge(sem, value)


def gnn(nc, x, src, dst, edge_attr, w1, b1, w2, b2, wout, bout, v1, c1, v2, c2, eps, out):
    N, D = x.shape
    E = src.shape[0]
    P = 128
    T = -(-E // P)
    G = T // 2
    assert T == 2 * G and G == R * R
    NG = -(-N // (4 * P))
    assert NG == 2 * G
    FULL = NG - 1
    LEFT = N - FULL * 4 * P
    LP, LJ = LEFT // 3, 3
    assert LP * LJ == LEFT and LP % 16 == 0
    ELEFT = E - (T - 1) * P
    NT = -(-(N + 3 * P) // P) * P
    U = D + 4
    L, LD = R - 1, RD - 1
    PRE = NG - 2 * RD * R
    FJ = 4 * NG
    A0_CHUNK, CHUNK = FJ // PRE, FJ // G
    assert FJ == A0_CHUNK * PRE == CHUNK * G and N <= P * FJ <= NT
    LN_EPS = 1e-5

    C = nc.dram_tensor("sums_a0_a1", (NT, 2 * U), F32).ap()
    A2 = nc.dram_tensor("sums_a2", (NT, D), F32).ap()
    Y = nc.dram_tensor("table_y", (NT, D), F32).ap()
    SRCROWS = nc.dram_tensor("src_as_float", (T, P), F32).ap()
    DSTROWS = nc.dram_tensor("dst_as_float", (T, P), F32).ap()
    C_units = C.rearrange("n (s u) -> (n s) u", s=2)
    C_filled = C[0:P * FJ].rearrange("(p j) (s u) -> p j s u", p=P, s=2)
    C_rest = C[P * FJ:NT].rearrange("(j p) u -> p j u", p=P)
    A2_filled = A2[0:P * FJ].rearrange("(p j) d -> p j d", p=P)
    A2_rest = A2[P * FJ:NT].rearrange("(j p) d -> p j d", p=P)

    def rows4(t):
        return t[0:FULL * 4 * P].rearrange("(g p j) d -> g p j d", p=P, j=4)

    def rows3(t):
        return t[FULL * 4 * P:N].rearrange("(p j) d -> p j d", j=LJ)

    x4, y4, a24, out4 = rows4(x), rows4(Y), rows4(A2), rows4(out)
    x3, y3, a23, out3 = rows3(x), rows3(Y), rows3(A2), rows3(out)
    rb_src = SRCROWS.rearrange("(g c) p -> g (c p)", c=2)
    rb_dst = DSTROWS.rearrange("(g c) p -> g (c p)", c=2)
    ea2 = edge_attr[0:(T - 2) * P].rearrange("(g c p) d -> g p c d", c=2, p=P)

    ctx = ExitStack()
    with ctx:
        def sb(name, shape, dt=F32):
            return ctx.enter_context(nc.sbuf_tensor(name, shape, dt))

        def ring(name, shape, dt=F32, slots=R):
            return [sb(f"{name}{i}", shape, dt) for i in range(slots)]

        def bank(name):
            return ctx.enter_context(nc.psum_tensor(name, [P, 512], F32))

        def sem(name):
            return ctx.enter_context(nc.semaphore(name))

        def sems(name, slots=R):
            return [sem(f"{name}{i}") for i in range(slots)]

        ident = sb("ident", [P, P])
        zeros = sb("zeros", [P, 2 * U])
        earlier = sb("earlier", [P, 2, 2 * P])
        spare_i = sb("spare_i", [P, 2], I32)
        spare = sb("spare", [P, 2])
        w1_sb, w2_sb, v1_sb, v2_sb = (sb(n, [P, D]) for n in ("w1s", "w2s", "v1s", "v2s"))
        wo_sb = sb("wos", [P, 2, D])
        b1_col, b2_col, c1_col, eps_col, eps1_col, ln_col = (sb(n, [P, 1]) for n in ("b1c", "b2c", "c1c", "epc", "ep1", "lnc"))
        b1_row, bo_row, c2_row = (sb(n, [P, D]) for n in ("b1r", "bor", "c2r"))
        rows_i = [sb(f"rows_i{n}", [T, P], I32) for n in range(2)]
        rows_f = [sb(f"rows_f{n}", [T, P]) for n in range(2)]
        raw = [sb(f"raw{n}", [P, T]) for n in range(2)]
        off_spare = [sb(f"offs{n}", [P, G, 2]) for n in range(2)]
        near = [sb(f"near{n}", [P, T]) for n in range(2)]
        src_i, dst_i, dst2_i = (sb(n, [P, T], I32) for n in ("src_i", "dst_i", "dst2_i"))
        to_a1 = sb("to_a1", [P, T], I32)
        to_y = sb("to_y", [P, T], I32)
        V = ring("V", [P, 2, U])
        UU = ring("U", [P, 2, U])
        S = ring("S", [P, 2, 2 * P])
        rb = ring("rb", [P, 2 * P])
        cs = ring("cs", [P, 2, 2 * U])
        xs = ring("xs", [P, 2, D])
        ea = ring("ea", [P, 2, D])
        ye = ring("ye", [P, 2, D])
        agg = ring("agg", [P, 2, D])
        gi = ring("gi", [P, 2], I32)
        si = ring("si", [P, 2], I32)
        yi = ring("yi", [P, 2], I32)
        xkeep = sb("xkeep", [P, G, 2, D])
        aggT, x1Te, s2T, x2Te = (sb(n, [P, 2 * P]) for n in ("aggT", "x1Te", "s2T", "x2Te"))
        pre, s1, s2, re, xbe = (sb(n, [P, 2, D]) for n in ("pre", "s1", "s2", "re", "xbe"))
        count, masked, row1 = (sb(n, [P, 2]) for n in ("count", "masked", "row1"))
        junk = sb("junk", [P, 2, 2 * P])
        deg, inv = (sb(n, [P, 2, 1]) for n in ("deg", "inv"))
        ste, mve, sde, rse = sb("ste", [P, 2, 6]), sb("mve", [P, 2, 2]), sb("sde", [P, 2]), sb("rse", [P, 2])
        xt = ring("xt", [P, 4, D], slots=RD)
        yd = ring("yd", [P, 4, D], slots=RD)
        ta = ring("ta", [P, 4, D], slots=RD)
        xT, x1T, x2T = (sb(n, [P, 4 * P]) for n in ("xT", "x1T", "x2T"))
        st = sb("st", [P, 4, 6])
        mv = ring("mv", [P, 4, 2], slots=RD)
        sd, rs, nm = (ring(n, [P, 4], slots=RD) for n in ("sd", "rs", "nm"))
        bT, bH, bY, bE1, bE2, bU = (bank(n) for n in ("bT", "bH", "bY", "bE1", "bE2", "bU"))

        rb_in, gathered, gathered2, added, y_put, ea_in = (
            sems(n) for n in ("rb_in", "gathered", "gathered2", "added", "y_put", "ea_in"))
        xt_in, y_out, ya_in, ta_in, out_out = (sems(n, RD) for n in ("xt_in", "y_out", "ya_in", "ta_in", "out_out"))
        w_in, idx_in, rows_out, fill_a0, fill_a1, fill_a2 = (
            sem(n) for n in ("w_in", "idx_in", "rows_out", "fill_a0", "fill_a1", "fill_a2"))
        (pool_c, pool_id, spare_ok, rows_ok, dve_c, rowsT, idx_ok, gi_ok, yi_ok, zeros_ok,
         v_ok, ln_ok) = (sem(n) for n in ("pool_c", "pool_id", "spare_ok", "rows_ok", "dve_c", "rowsT", "idx_ok",
                                          "gi_ok", "yi_ok", "zeros_ok", "v_ok", "ln_ok"))
        (pT, p1, p2, pY, aT, a1, a2, aS, aN, dX, dR, dSt, dMv, dRs, dNm) = (sem(n) for n in (
            "pT", "p1", "p2", "pY", "aT", "a1", "a2", "aS", "aN", "dX", "dR", "dSt", "dMv", "dRs", "dNm"))
        (dS, dCount, dMask, dRow, dSi, pU, aU, aKeep) = (sem(n) for n in (
            "dS", "dCount", "dMask", "dRow", "dSi", "pU", "aU", "aKeep"))
        (dDeg, dInv, dAgg, pTe, aTe, pXe, dPre, aV) = (sem(n) for n in (
            "dDeg", "dInv", "dAgg", "pTe", "aTe", "pXe", "dPre", "aV"))
        (p1e, a1e, pT2, dS1, dS2, pT3, aT3, p2e, a2e, pYe, dXe, dRe, dSte, dMve, aSe, dRse, dNe, dM) = (sem(n) for n in (
            "p1e", "a1e", "pT2", "dS1", "dS2", "pT3", "aT3", "p2e", "a2e", "pYe", "dXe", "dRe", "dSte", "dMve", "aSe",
            "dRse", "dNe", "dM"))
        (oH, oTp, oTc, oM1, oR1, oM2, oB, oR, oSt, oMv, oSd, oRs, oNm, oN) = (sem(n) for n in (
            "oH", "oTp", "oTc", "oM1", "oR1", "oM2", "oB", "oR", "oSt", "oMv", "oSd", "oRs", "oNm", "oN"))

        waited = sem("waited")
        W_LOADS = 12
        block = ctx.enter_context(nc.Block())

        def dims(g):
            return (LP, LJ) if g.is_any(NG - 1) else (P, 4)

        def seq(ph, s):
            return G * ph + s.k

        def dense_of(ph, s):
            if s.slot >= RD:
                return None
            return At(RD, s.i, PRE + RD * R * ph + RD * (s.off // R) + s.slot)

        def stand_alone(eng):
            eng.sem_inc(waited, 1)

        @block.sync
        def _(sp):
            sp.wait_ge(rows_ok, 2)
            for n, idx in enumerate((src, dst)):
                sp.dma_start(rows_i[n][0:T - 1, :], idx[0:(T - 1) * P].rearrange("(t p) -> t p", p=P)).then_inc(idx_in, 16)
                sp.dma_start(rows_i[n][T - 1:T, 0:ELEFT],
                             idx[(T - 1) * P:E].rearrange("(t p) -> t p", t=1)).then_inc(idx_in, 16)
            for dest, source in ((w1_sb[:, :], w1), (w2_sb[:, :], w2), (v1_sb[:, :], v1), (v2_sb[:, :], v2),
                                 (wo_sb[:, :, :], wout.rearrange("(h p) d -> p h d", h=2)),
                                 (b1_col[:, :], b1.rearrange("(p o) -> p o", o=1)),
                                 (b2_col[:, :], b2.rearrange("(p o) -> p o", o=1)),
                                 (c1_col[:, :], c1.rearrange("(p o) -> p o", o=1)),
                                 (b1_row[:, :], b1.partition_broadcast(P)),
                                 (bo_row[:, :], bout.partition_broadcast(P)),
                                 (c2_row[:, :], c2.partition_broadcast(P)),
                                 (eps_col[:, :], eps.partition_broadcast(P))):
                sp.dma_start(dest, source).then_inc(w_in, 16)

            def load_x(g):
                if g.is_any(NG - 1):
                    sp.dma_start(xt[g.slot][0:LP, 0:LJ, :], x3).then_inc(xt_in[g.slot], 16)
                else:
                    sp.dma_start(xt[g.slot][:, :, :], x4[g.k]).then_inc(xt_in[g.slot], 16)

            def store_y(g):
                wait(sp, aN, g.k + 1)
                if g.is_any(NG - 1):
                    sp.dma_start(y3, yd[g.slot][0:LP, 0:LJ, :]).then_inc(y_out[g.slot], 16)
                else:
                    sp.dma_start(y4[g.k], yd[g.slot][:, :, :]).then_inc(y_out[g.slot], 16)

            def dense_step(g):
                if not g.is_from(NG - LD):
                    wait(sp, dR, g.k)
                    load_x(g.at(LD))
                if not g.is_any(0, 1):
                    store_y(g.at(-2))

            for k in range(LD):
                load_x(dense(k))
            sp.wait_ge(dve_c, 2)
            sp.dma_start(SRCROWS, rows_f[0][:, :]).then_inc(rows_out, 16)
            sp.dma_start(DSTROWS, rows_f[1][:, :]).then_inc(rows_out, 16)

            sp.wait_ge(zeros_ok, 1)
            sp.dma_start(C_rest, zeros[:, 0:2 * U].unsqueeze(1).broadcast_to([P, NT // P - FJ, 2 * U])).then_inc(fill_a0, 16)
            for k in range(PRE):
                sp.dma_start(C_filled[:, A0_CHUNK * k:A0_CHUNK * (k + 1), 0, :],
                             zeros[:, 0:U].unsqueeze(1).broadcast_to([P, A0_CHUNK, U])).then_inc(fill_a0, 16)
                dense_step(dense(k))
            sp.dma_start(A2_rest, zeros[:, 0:D].unsqueeze(1).broadcast_to([P, NT // P - FJ, D])).then_inc(fill_a2, 16)
            sp.wait_ge(rows_out, 32)

            def load_rb(ph, d):
                table = rb_dst if ph == 2 else rb_src
                sp.dma_start(rb[d.slot][:, :], table[d.k].partition_broadcast(P)).then_inc(rb_in[d.slot], 16)

            def zeros_a1(s):
                sp.dma_start(C_filled[:, bass.ds(CHUNK * s.k, CHUNK), 1, :],
                             zeros[:, 0:U].unsqueeze(1).broadcast_to([P, CHUNK, U])).then_inc(fill_a1, 16)

            def zeros_a2(s):
                sp.dma_start(A2_filled[:, bass.ds(CHUNK * s.k, CHUNK), :],
                             zeros[:, 0:D].unsqueeze(1).broadcast_to([P, CHUNK, D])).then_inc(fill_a2, 16)

            for ph in range(2):
                wait(sp, dS, G * ph)
                for k in range(L):
                    load_rb(ph, edge(k))

                def step(s, ph=ph):
                    if not s.is_from(G - L):
                        wait(sp, dS, seq(ph, s))
                        load_rb(ph, s.at(L))
                    if g := dense_of(ph, s):
                        dense_step(g)
                    (zeros_a1, zeros_a2)[ph](s)

                steps(sp, step, R, G)
            store_y(dense(NG - 2))
            store_y(dense(NG - 1))

            def load_ea(d):
                if d.is_any(G - 1):
                    sp.dma_start(ea[d.slot][:, 0, :], edge_attr[(T - 2) * P:(T - 1) * P]).then_inc(ea_in[d.slot], 16)
                    sp.dma_start(ea[d.slot][0:ELEFT, 1, :], edge_attr[(T - 1) * P:E]).then_inc(ea_in[d.slot], 16)
                else:
                    sp.dma_start(ea[d.slot][:, :, :], ea2[d.k]).then_inc(ea_in[d.slot], 16)

            sp.wait_ge(dS, 2 * G)
            for k in range(L):
                load_rb(2, edge(k))
                load_ea(edge(k))

            def step2(s):
                if not s.is_from(G - L):
                    wait(sp, dS, seq(2, s))
                    load_rb(2, s.at(L))
                    wait(sp, dM, s.k)
                    load_ea(s.at(L))

            steps(sp, step2, R, G)

            for n in range(R):
                sp.wait_ge(y_put[n], 32 * R)
                sp.wait_ge(added[n], 32 * 3 * R)

            def load_ya(g):
                if g.is_any(NG - 1):
                    sp.dma_start(xt[g.slot][0:LP, 0:LJ, :], y3).then_inc(ya_in[g.slot], 16)
                    sp.dma_start(ta[g.slot][0:LP, 0:LJ, :], a23).then_inc(ta_in[g.slot], 16)
                else:
                    sp.dma_start(xt[g.slot][:, :, :], y4[g.k]).then_inc(ya_in[g.slot], 16)
                    sp.dma_start(ta[g.slot][:, :, :], a24[g.k]).then_inc(ta_in[g.slot], 16)

            def store_out(g):
                wait(sp, oN, g.k + 1)
                if g.is_any(NG - 1):
                    sp.dma_start(out3, yd[g.slot][0:LP, 0:LJ, :]).then_inc(out_out[g.slot], 16)
                else:
                    sp.dma_start(out4[g.k], yd[g.slot][:, :, :]).then_inc(out_out[g.slot], 16)

            for k in range(LD):
                load_ya(dense(k))

            def step3(g):
                if not g.is_from(NG - LD):
                    wait(sp, oTp, g.k)
                    wait(sp, oR, g.k)
                    load_ya(g.at(LD))
                if not g.is_any(0, 1):
                    store_out(g.at(-2))

            steps(sp, step3, RD, NG)
            store_out(dense(NG - 2))
            store_out(dense(NG - 1))
            for n in range(RD):
                sp.wait_ge(out_out[n], 16 * len(range(n, NG, RD)))

        @block.gpsimd
        def _(pool):
            for n in range(2):
                nc.gpsimd.iota(rows_i[n][:, :], [[1, P]], base=N + 2 * P, channel_multiplier=0).then_inc(rows_ok, 1)
            nc.gpsimd.memset(ident[:, :], 0.0).then_inc(pool_c, 1)
            nc.gpsimd.memset(earlier[:, :, :], 1.0).then_inc(pool_c, 1)
            nc.gpsimd.iota(spare_i[:, :], [[P, 2]], base=N, channel_multiplier=1).then_inc(spare_ok, 1)
            pool.wait_ge(pool_c, 2)
            nc.gpsimd.affine_select(out=ident[:, :], in_=ident[:, :], compare_op=ALU.not_equal, fill=1.0, base=0,
                                    pattern=[[-1, P]], channel_multiplier=1).then_inc(pool_id, 1)
            nc.gpsimd.affine_select(out=earlier[:, :, :], in_=earlier[:, :, :], compare_op=ALU.is_gt, fill=0.0, base=0,
                                    pattern=[[P, 2], [-1, 2 * P]], channel_multiplier=1).then_inc(pool_id, 1)

            def copy_gi(ph, d):
                table = (dst_i, dst2_i, src_i)[ph]
                if ph == 2:
                    wait(pool, gathered2[d.slot], 64 * d.lap)
                    if d.is_any(*range(R)):
                        pool.wait_ge(gathered[d.slot], 32 * 2 * R)
                else:
                    wait(pool, gathered[d.slot], 32 * (R * ph + d.lap))
                nc.gpsimd.tensor_copy(gi[d.slot][:, :], table[:, bass.ds(2 * d.k, 2)]).then_inc(gi_ok, 1)

            def rows_of(index, c):
                return bass.IndirectOffsetOnAxis(ap=index[:, c:c + 1], axis=0)

            def gather(ph, d):
                wait(pool, gi_ok, seq(ph, d) + 1)
                stand_alone(pool)
                for c in range(2):
                    if ph == 0:
                        pool.indirect_dma_start(out=V[d.slot][:, c, 0:D], out_offset=None, in_=x,
                                                in_offset=rows_of(gi[d.slot], c)).then_inc(gathered[d.slot], 16)
                    elif ph == 1:
                        pool.indirect_dma_start(out=cs[d.slot][:, c, 0:U], out_offset=None, in_=C_units,
                                                in_offset=rows_of(gi[d.slot], c)).then_inc(gathered[d.slot], 16)
                    else:
                        pool.indirect_dma_start(out=cs[d.slot][:, c, :], out_offset=None, in_=C,
                                                in_offset=rows_of(gi[d.slot], c)).then_inc(gathered2[d.slot], 16)
                        pool.indirect_dma_start(out=xs[d.slot][:, c, :], out_offset=None, in_=x,
                                                in_offset=rows_of(gi[d.slot], c)).then_inc(gathered2[d.slot], 16)

            def add_rows(ph, s, index):
                wait(pool, aU, seq(ph, s) + 1)
                if not (ph == 0 and s.is_any(0)):
                    b = s.at(-1)
                    wait(pool, added[b.slot], 32 * (R * ph + b.lap + 1))
                stand_alone(pool)
                for c in range(2):
                    pool.indirect_dma_start(out=A2 if ph == 2 else C_units, out_offset=rows_of(index, c),
                                            in_=UU[s.slot][:, c, 0:D] if ph == 2 else UU[s.slot][:, c, :], in_offset=None,
                                            compute_op=ALU.add).then_inc(added[s.slot], 16)

            pool.wait_ge(idx_ok, 2)
            pool.wait_ge(v_ok, 1)
            for ph in range(2):
                if ph == 1:
                    pool.wait_ge(added[(G - 1) % R], 32 * R)
                copy_gi(ph, edge(0))
                for k in range(L):
                    gather(ph, edge(k))
                    copy_gi(ph, edge(k + 1))
                if ph == 0:
                    pool.wait_ge(fill_a0, 16 * (PRE + 1))
                else:
                    pool.wait_ge(fill_a1, 16 * G)

                def step(s, ph=ph):
                    if not s.is_from(G - L):
                        if ph == 0:
                            wait(pool, pU, s.k)
                            wait(pool, aKeep, s.k)
                        else:
                            wait(pool, dAgg, s.k)
                        gather(ph, s.at(L))
                        if not s.is_from(G - L - 1):
                            copy_gi(ph, s.at(L + 1))
                    if ph == 1:
                        nc.gpsimd.tensor_copy(si[s.slot][:, :], to_a1[:, bass.ds(2 * s.k, 2)]).then_inc(yi_ok, 1)
                        wait(pool, yi_ok, s.k + 1)
                    else:
                        wait(pool, dSi, s.k + 1)
                    add_rows(ph, s, si[s.slot])

                steps(pool, step, R, G)

            pool.wait_ge(added[(G - 1) % R], 32 * 2 * R)
            copy_gi(2, edge(0))
            for k in range(L):
                gather(2, edge(k))
                copy_gi(2, edge(k + 1))
            pool.wait_ge(fill_a2, 16 * (G + 1))
            for n in range(RD):
                pool.wait_ge(y_out[n], 16 * len(range(n, NG, RD)))

            def put(b):
                wait(pool, dNe, b.k + 1)
                wait(pool, yi_ok, G + b.k + 1)
                if not b.is_any(0):
                    a = b.at(-1)
                    wait(pool, y_put[a.slot], 32 * (a.lap + 1))
                stand_alone(pool)
                for c in range(2):
                    pool.indirect_dma_start(out=Y, out_offset=rows_of(yi[b.slot], c), in_=ye[b.slot][:, c, :],
                                            in_offset=None).then_inc(y_put[b.slot], 16)
                wait(pool, dSi, G + b.k + 1)
                add_rows(2, b, si[b.slot])

            def step2(s):
                nc.gpsimd.tensor_copy(yi[s.slot][:, :], to_y[:, bass.ds(2 * s.k, 2)]).then_inc(yi_ok, 1)
                if not s.is_any(0):
                    put(s.at(-1))
                if not s.is_from(G - L):
                    wait(pool, dRe, s.k)
                    gather(2, s.at(L))
                    if not s.is_from(G - L - 1):
                        copy_gi(2, s.at(L + 1))

            steps(pool, step2, R, G)
            put(edge(G - 1))

            def step3(g):
                p, j = dims(g)
                wait(pool, oH, g.k + 1)
                nc.gpsimd.tensor_tensor(xt[g.slot][0:p, 0:j, :], xt[g.slot][0:p, 0:j, :],
                                        c2_row[0:p, :].unsqueeze(1).broadcast_to([p, j, D]), ALU.add).then_inc(oB, 1)

            steps(pool, step3, RD, NG)

        @block.scalar
        def _(act):
            def copy_xT(g):
                p, j = dims(g)
                wait(act, pT, g.k + 1)
                wait(act, p1, g.k)
                nc.scalar.activation(xT[:, 0:p * j], bT[:, 0:p * j], ACT.Copy).then_inc(aT, 1)

            def root(g, moments, done):
                wait(act, moments, g.k + 1)
                p, j = dims(g)
                nc.scalar.activation(sd[g.slot][0:p, 0:j], mv[g.slot][0:p, 0:j, 1], ACT.Sqrt,
                                     bias=ln_col[0:p, :]).then_inc(done, 1)

            def scale(g, ready, done):
                p, j = dims(g)
                wait(act, ready, g.k + 1)
                for q in range(j):
                    ins = nc.scalar.activation(yd[g.slot][0:p, q, :], yd[g.slot][0:p, q, :], ACT.Identity,
                                               scale=rs[g.slot][0:p, q:q + 1], bias=nm[g.slot][0:p, q:q + 1])
                ins.then_inc(done, 1)

            def dense_1(g):
                p, j = dims(g)
                wait(act, p1, g.k + 1)
                wait(act, pY, g.k)
                nc.scalar.activation(x1T[:, 0:p * j], bH[:, 0:p * j], ACT.Relu, bias=b1_col[:, :]).then_inc(a1, 1)
                if not g.is_any(NG - 1):
                    copy_xT(g.at(1))
                if not g.is_any(0, 1):
                    scale(g.at(-2), dNm, aN)

            def dense_2(g):
                p, j = dims(g)
                wait(act, p2, g.k + 1)
                nc.scalar.activation(x2T[:, 0:p * j], bH[:, 0:p * j], ACT.Relu, bias=b2_col[:, :]).then_inc(a2, 1)
                if not g.is_any(0):
                    root(g.at(-1), dMv, aS)

            act.wait_ge(w_in, 16 * W_LOADS)
            act.wait_ge(ln_ok, 1)
            copy_xT(dense(0))
            for k in range(PRE):
                dense_1(dense(k))
                dense_2(dense(k))

            for ph in range(2):
                def step(s, ph=ph):
                    g = dense_of(ph, s)
                    if g:
                        dense_1(g)
                    if ph == 0:
                        wait(act, gathered[s.slot], 32 * (s.lap + 1))
                        nc.scalar.activation(xkeep[:, bass.ds(s.k, 1), :, :].rearrange("p a c d -> p (a c) d"),
                                             V[s.slot][:, :, 0:D], ACT.Copy).then_inc(aKeep, 1)
                    else:
                        wait(act, pTe, s.k + 1)
                        wait(act, pXe, s.k)
                        nc.scalar.activation(aggT[:, :], bE1[:, 0:2 * P], ACT.Copy).then_inc(aTe, 1)
                    if g:
                        dense_2(g)
                    if ph == 1:
                        wait(act, dPre, s.k + 1)
                        nc.scalar.activation(V[s.slot][:, :, 0:D], pre[:, :, :], ACT.Relu).then_inc(aV, 1)
                    wait(act, pU, seq(ph, s) + 1)
                    wait(act, added[s.slot], 32 * (R * ph + s.lap))
                    nc.scalar.activation(UU[s.slot][:, :, :], bU[:, 0:2 * U].rearrange("p (c u) -> p c u", c=2),
                                         ACT.Copy).then_inc(aU, 1)

                steps(act, step, R, G)
            scale(dense(NG - 2), dNm, aN)
            root(dense(NG - 1), dMv, aS)
            scale(dense(NG - 1), dNm, aN)

            def first(s):
                wait(act, pTe, G + s.k + 1)
                wait(act, p1e, s.k)
                nc.scalar.activation(aggT[:, :], bE1[:, 0:2 * P], ACT.Copy).then_inc(aTe, 1)
                wait(act, p1e, s.k + 1)
                wait(act, pYe, s.k)
                nc.scalar.activation(x1Te[:, :], bH[:, 0:2 * P], ACT.Relu, bias=b1_col[:, :]).then_inc(a1e, 1)

            def second(b):
                wait(act, dMve, b.k + 1)
                nc.scalar.activation(sde[:, :], mve[:, :, 1], ACT.Sqrt, bias=ln_col[:, :]).then_inc(aSe, 1)

            def third(s):
                wait(act, pT3, s.k + 1)
                wait(act, p2e, s.k)
                nc.scalar.activation(s2T[:, :], bT[:, 0:2 * P], ACT.Copy).then_inc(aT3, 1)
                wait(act, p2e, s.k + 1)
                nc.scalar.activation(x2Te[:, :], bH[:, 0:2 * P], ACT.Relu, bias=b2_col[:, :]).then_inc(a2e, 1)

            def fourth(b):
                wait(act, dM, b.k + 1)
                nc.scalar.activation(V[b.slot][:, :, 0:D], pre[:, :, :], ACT.Relu).then_inc(aV, 1)
                wait(act, pU, 2 * G + b.k + 1)
                wait(act, added[b.slot], 32 * (2 * R + b.lap))
                nc.scalar.activation(UU[b.slot][:, :, 0:D], bU[:, 0:2 * D].rearrange("p (c u) -> p c u", c=2),
                                     ACT.Copy).then_inc(aU, 1)

            def step2(s):
                first(s)
                if not s.is_any(0):
                    second(s.at(-1))
                third(s)
                if not s.is_any(0):
                    fourth(s.at(-1))

            steps(act, step2, R, G)
            second(edge(G - 1))
            fourth(edge(G - 1))

            def copy_hT(g):
                p, j = dims(g)
                wait(act, oTp, g.k + 1)
                wait(act, oM1, g.k)
                nc.scalar.activation(xT[:, 0:p * j], bT[:, 0:p * j], ACT.Copy).then_inc(oTc, 1)

            copy_hT(dense(0))

            def step3(g):
                p, j = dims(g)
                wait(act, oM1, g.k + 1)
                wait(act, oM2, g.k)
                nc.scalar.activation(x1T[:, 0:p * j], bH[:, 0:p * j], ACT.Relu, bias=c1_col[:, :]).then_inc(oR1, 1)
                if not g.is_any(NG - 1):
                    copy_hT(g.at(1))
                if not g.is_any(0, 1):
                    scale(g.at(-2), oNm, oN)
                if not g.is_any(0):
                    root(g.at(-1), oMv, oSd)

            steps(act, step3, RD, NG)
            scale(dense(NG - 2), oNm, oN)
            root(dense(NG - 1), oMv, oSd)
            scale(dense(NG - 1), oNm, oN)

        @block.vector
        def _(dve):
            v = nc.vector
            v.memset(zeros[:, :], 0.0).then_inc(zeros_ok, 1)
            v.memset(ln_col[:, :], LN_EPS).then_inc(ln_ok, 1)
            for n in range(R):
                ins = v.memset(V[n][:, :, D:U], 1.0)
            ins.then_inc(v_ok, 1)
            dve.wait_ge(idx_in, 64)
            for n in range(2):
                v.tensor_copy(rows_f[n][:, :], rows_i[n][:, :]).then_inc(dve_c, 1)
            dve.wait_ge(spare_ok, 1)
            v.tensor_copy(spare[:, :], spare_i[:, :]).then_inc(dve_c, 1)
            dve.wait_ge(rowsT, 1)
            for n, b in enumerate((bE1, bE2)):
                v.tensor_copy(raw[n][:, :], b[:, 0:T]).then_inc(dve_c, 1)
            dve.wait_ge(dve_c, 5)
            for n in range(2):
                v.tensor_scalar(near[n][:, :], raw[n][:, :], float(N - 1), None, ALU.min).then_inc(dve_c, 1)
                v.tensor_tensor(off_spare[n][:, :, :], raw[n][:, :].rearrange("p (g c) -> p g c", c=2),
                                spare[:, :].unsqueeze(1).broadcast_to([P, G, 2]), ALU.subtract).then_inc(dve_c, 1)
            dve.wait_ge(dve_c, 9)
            v.tensor_copy(src_i[:, :], near[0][:, :])
            v.tensor_scalar(dst2_i[:, :], near[1][:, :], 2.0, None, ALU.mult)
            v.tensor_copy(dst_i[:, :], near[1][:, :]).then_inc(idx_ok, 1)
            dve.wait_ge(w_in, 16 * W_LOADS)
            v.tensor_scalar(eps1_col[:, :], eps_col[:, :], 1.0, None, ALU.add).then_inc(idx_ok, 1)

            def moments(g, product, other, summed, stats, done):
                p, j = dims(g)
                wait(dve, product, g.k + 1)
                wait(dve, other, g.k + 1)
                v.tensor_tensor(yd[g.slot][0:p, 0:j, :], bY[0:p, 0:j * D].rearrange("p (j d) -> p j d", j=j),
                                xt[g.slot][0:p, 0:j, :], ALU.add).then_inc(summed, 1)
                wait(dve, summed, g.k + 1)
                wait(dve, done, g.k)
                for q in range(j):
                    ins = v.bn_stats(st[0:p, q, :], yd[g.slot][0:p, q, :])
                ins.then_inc(stats, 1)
                wait(dve, stats, g.k + 1)
                stand_alone(dve)
                for q in range(j):
                    ins = v.bn_aggr(mv[g.slot][0:p, q, :], st[0:p, q, :])
                ins.then_inc(done, 1)

            def factors(g, rooted, inverted, done):
                p, j = dims(g)
                wait(dve, rooted, g.k + 1)
                v.reciprocal(rs[g.slot][0:p, 0:j], sd[g.slot][0:p, 0:j]).then_inc(inverted, 1)
                wait(dve, inverted, g.k + 1)
                v.scalar_tensor_tensor(out=nm[g.slot][0:p, 0:j], in0=mv[g.slot][0:p, 0:j, 0], scalar=-1.0,
                                       in1=rs[g.slot][0:p, 0:j], op0=ALU.mult, op1=ALU.mult).then_inc(done, 1)

            def dense_moments(g):
                wait(dve, y_out[g.slot], 16 * g.lap)
                moments(g, pY, dX, dR, dSt, dMv)

            def dense_1(g):
                if not g.is_any(0):
                    dense_moments(g.at(-1))
                p, j = dims(g)
                wait(dve, pT, g.k + 1)
                v.tensor_tensor(xt[g.slot][0:p, 0:j, :], xt[g.slot][0:p, 0:j, :],
                                bo_row[0:p, :].unsqueeze(1).broadcast_to([p, j, D]), ALU.add).then_inc(dX, 1)

            def dense_2(g):
                if not g.is_any(0):
                    factors(g.at(-1), aS, dRs, dNm)

            def equalities(ph, d, presums):
                which = 1 if ph == 2 else 0
                wait(dve, rb_in[d.slot], 16 * (R * ph + d.lap + 1))
                wait(dve, pU, presums)
                for c in range(2):
                    ins = v.tensor_scalar(S[d.slot][:, c, :], rb[d.slot][:, :], raw[which][:, bass.ds(2 * d.k + c, 1)], None,
                                          ALU.is_equal)
                ins.then_inc(dS, 1)
                if ph == 1:
                    return
                n = (G if ph == 2 else 0) + d.k + 1
                wait(dve, dS, G * ph + d.k + 1)
                wait(dve, dSi, n - 1)
                for c in range(2):
                    ins = v.tensor_tensor_reduce(out=junk[:, c, :], in0=S[d.slot][:, c, :], in1=earlier[:, c, :], scale=1.0,
                                                 scalar=0.0, op0=ALU.mult, op1=ALU.add, accum_out=count[:, c:c + 1])
                ins.then_inc(dCount, 1)
                wait(dve, dCount, n)
                v.scalar_tensor_tensor(out=masked[:, :], in0=count[:, :], scalar=0.0,
                                       in1=off_spare[which][:, bass.ds(d.k, 1), :].rearrange("p a c -> p (a c)"),
                                       op0=ALU.is_equal, op1=ALU.mult).then_inc(dMask, 1)
                wait(dve, dMask, n)
                v.tensor_tensor(row1[:, :], masked[:, :], spare[:, :], ALU.add).then_inc(dRow, 1)
                wait(dve, dRow, n)
                wait(dve, added[d.slot], 32 * (R * ph + d.lap))
                if ph == 0:
                    v.tensor_scalar(to_a1[:, bass.ds(2 * d.k, 2)], row1[:, :], 2.0, 1.0, ALU.mult, ALU.add)
                    v.tensor_copy(to_y[:, bass.ds(2 * d.k, 2)], row1[:, :])
                v.tensor_scalar(si[d.slot][:, :], row1[:, :], 2.0 if ph == 0 else 1.0, None, ALU.mult).then_inc(dSi, 1)

            def mean(n, d, total):
                wait(dve, dAgg, n - 1)
                v.tensor_tensor(agg[d.slot][:, :, :], total, cs[d.slot][:, :, 0:D], ALU.add)
                v.tensor_scalar(deg[:, :, :], cs[d.slot][:, :, D:D + 1], 1.0, 1.0, ALU.add, ALU.max).then_inc(dDeg, 1)
                wait(dve, dDeg, n)
                v.reciprocal(inv[:, :, :], deg[:, :, :]).then_inc(dInv, 1)
                wait(dve, dInv, n)
                v.tensor_tensor(agg[d.slot][:, :, :], agg[d.slot][:, :, :], inv[:, :, :].broadcast_to([P, 2, D]),
                                ALU.mult).then_inc(dAgg, 1)

            def mean1(d):
                wait(dve, gathered[d.slot], 32 * (R + d.lap + 1))
                mean(d.k + 1, d, xkeep[:, bass.ds(d.k, 1), :, :].rearrange("p a c d -> p (a c) d"))

            def mean2(d):
                wait(dve, gathered2[d.slot], 64 * (d.lap + 1))
                wait(dve, dS2, d.k)
                mean(G + d.k + 1, d, xs[d.slot][:, :, :])

            for k in range(PRE):
                dense_1(dense(k))
                dense_2(dense(k))

            for ph in range(2):
                equalities(ph, edge(0), G * ph)
                if ph == 1:
                    dve.wait_ge(aKeep, G)
                    mean1(edge(0))

                def step(s, ph=ph):
                    g = dense_of(ph, s)
                    if g:
                        dense_1(g)
                    if ph == 1:
                        wait(dve, pXe, s.k + 1)
                        wait(dve, aV, s.k)
                        v.tensor_tensor(pre[:, :, :], bE2[:, 0:2 * D].rearrange("p (c d) -> p c d", c=2),
                                        b1_row[:, :].unsqueeze(1).broadcast_to([P, 2, D]), ALU.add).then_inc(dPre, 1)
                        if not s.is_any(G - 1):
                            mean1(s.at(1))
                    if not s.is_any(G - 1):
                        equalities(ph, s.at(1), seq(ph, s))
                    if g:
                        dense_2(g)

                steps(dve, step, R, G)
            dense_moments(dense(NG - 1))
            factors(dense(NG - 1), aS, dRs, dNm)

            equalities(2, edge(0), 2 * G)
            mean2(edge(0))

            def moments2(b):
                n = b.k + 1
                wait(dve, dM, b.k)
                wait(dve, pYe, n)
                wait(dve, dXe, n)
                v.tensor_tensor(re[:, :, :], bY[:, 0:2 * D].rearrange("p (c d) -> p c d", c=2), xbe[:, :, :],
                                ALU.add).then_inc(dRe, 1)
                wait(dve, dRe, n)
                for c in range(2):
                    ins = v.bn_stats(ste[:, c, :], re[:, c, :])
                ins.then_inc(dSte, 1)
                wait(dve, dSte, n)
                stand_alone(dve)
                for c in range(2):
                    ins = v.bn_aggr(mve[:, c, :], ste[:, c, :])
                ins.then_inc(dMve, 1)

            def message(b):
                n = b.k + 1
                wait(dve, aSe, n)
                v.reciprocal(rse[:, :], sde[:, :]).then_inc(dRse, 1)
                wait(dve, dRse, n)
                wait(dve, y_put[b.slot], 32 * b.lap)
                for c in range(2):
                    ins = v.tensor_scalar(ye[b.slot][:, c, :], re[:, c, :], mve[:, c, 0:1], rse[:, c:c + 1],
                                          ALU.subtract, ALU.mult)
                ins.then_inc(dNe, 1)
                wait(dve, dNe, n)
                wait(dve, ea_in[b.slot], 16 * (b.lap + 1) + (16 if b.is_any(G - 1) else 0))
                wait(dve, aV, G + b.k)
                v.tensor_tensor(pre[:, :, :], ye[b.slot][:, :, :], ea[b.slot][:, :, :], ALU.add).then_inc(dM, 1)

            def step2(s):
                if not s.is_any(0):
                    moments2(s.at(-1))
                wait(dve, dRe, s.k)
                v.tensor_tensor(xbe[:, :, :], xs[s.slot][:, :, :], bo_row[:, :].unsqueeze(1).broadcast_to([P, 2, D]),
                                ALU.add).then_inc(dXe, 1)
                wait(dve, dS2, s.k)
                wait(dve, pT2, s.k + 1)
                v.tensor_tensor(s1[:, :, :], bE2[:, 0:2 * D].rearrange("p (c d) -> p c d", c=2),
                                cs[s.slot][:, :, U:U + D], ALU.add).then_inc(dS1, 1)
                wait(dve, dS1, s.k + 1)
                wait(dve, pT3, s.k)
                v.tensor_tensor(s2[:, :, :], s1[:, :, :], inv[:, :, :].broadcast_to([P, 2, D]), ALU.mult).then_inc(dS2, 1)
                if not s.is_any(0):
                    message(s.at(-1))
                if not s.is_any(G - 1):
                    mean2(s.at(1))
                    equalities(2, s.at(1), 2 * G - 1 + s.k)

            steps(dve, step2, R, G)
            moments2(edge(G - 1))
            message(edge(G - 1))

            def sum3(g):
                p, j = dims(g)
                wait(dve, ya_in[g.slot], 16 * (g.lap + 1))
                wait(dve, ta_in[g.slot], 16 * (g.lap + 1))
                v.scalar_tensor_tensor(out=ta[g.slot][0:p, 0:j, :], in0=xt[g.slot][0:p, 0:j, :], scalar=eps1_col[0:p, 0:1],
                                       in1=ta[g.slot][0:p, 0:j, :], op0=ALU.mult, op1=ALU.add).then_inc(oH, 1)

            def moments3(g):
                wait(dve, out_out[g.slot], 16 * g.lap)
                moments(g, oM2, oB, oR, oSt, oMv)

            sum3(dense(0))
            sum3(dense(1))

            def step3(g):
                if not g.is_any(0):
                    moments3(g.at(-1))
                if not g.is_from(NG - 2):
                    sum3(g.at(2))
                if not g.is_any(0):
                    factors(g.at(-1), oSd, oRs, oNm)

            steps(dve, step3, RD, NG)
            moments3(dense(NG - 1))
            factors(dense(NG - 1), oSd, oRs, oNm)

        @block.tensor
        def _(pe):
            mm = nc.tensor.matmul

            def transpose_x(g):
                p, j = dims(g)
                wait(pe, xt_in[g.slot], 16 * (g.lap + 1))
                wait(pe, aT, g.k)
                for q in range(j):
                    ins = nc.tensor.transpose(bT[:, q * p:(q + 1) * p], xt[g.slot][0:p, q, :], ident[0:p, 0:p])
                ins.then_inc(pT, 1)

            def dense_1(g):
                p, j = dims(g)
                wait(pe, aT, g.k + 1)
                wait(pe, a2, g.k)
                mm(bH[:, 0:p * j], w1_sb[:, :], xT[:, 0:p * j], start=True, stop=True).then_inc(p1, 1)
                if not g.is_any(NG - 1):
                    transpose_x(g.at(1))

            def dense_2(g):
                p, j = dims(g)
                wait(pe, a1, g.k + 1)
                mm(bH[:, 0:p * j], w2_sb[:, :], x1T[:, 0:p * j], start=True, stop=True).then_inc(p2, 1)

            def dense_3(g):
                p, j = dims(g)
                wait(pe, a2, g.k + 1)
                wait(pe, dR, g.k)
                for q in range(j):
                    for h, t in enumerate((x1T, x2T)):
                        ins = mm(bY[0:p, q * D:(q + 1) * D], t[:, q * p:(q + 1) * p], wo_sb[:, h, :],
                                 start=(h == 0), stop=(h == 1))
                ins.then_inc(pY, 1)

            def sum_equal(s, width):
                for a in range(2):
                    for b in range(2):
                        ins = mm(bU[:, a * width:(a + 1) * width], S[s.slot][:, b, a * P:(a + 1) * P],
                                 V[s.slot][:, b, 0:width], start=(b == 0), stop=(b == 1))
                ins.then_inc(pU, 1)

            pe.wait_ge(pool_id, 2)
            pe.wait_ge(dve_c, 2)
            for n, b in enumerate((bE1, bE2)):
                ins = nc.tensor.transpose(b[:, 0:T], rows_f[n][:, :], ident[0:T, 0:T])
            ins.then_inc(rowsT, 1)
            pe.wait_ge(w_in, 16 * W_LOADS)
            transpose_x(dense(0))
            for k in range(PRE):
                dense_1(dense(k))
                dense_2(dense(k))
                dense_3(dense(k))

            for ph in range(2):
                def step(s, ph=ph):
                    g = dense_of(ph, s)
                    if g:
                        dense_1(g)
                    if ph == 0:
                        wait(pe, gathered[s.slot], 32 * (s.lap + 1))
                        wait(pe, dS, seq(ph, s) + 1)
                        wait(pe, aU, seq(ph, s))
                        sum_equal(s, U)
                    else:
                        wait(pe, dAgg, s.k + 1)
                        wait(pe, aTe, s.k)
                        for c in range(2):
                            ins = nc.tensor.transpose(bE1[:, c * P:(c + 1) * P], agg[s.slot][:, c, :], ident[:, :])
                        ins.then_inc(pTe, 1)
                    if g:
                        dense_2(g)
                    if ph == 1:
                        wait(pe, aTe, s.k + 1)
                        wait(pe, dPre, s.k)
                        for c in range(2):
                            ins = mm(bE2[:, c * D:(c + 1) * D], aggT[:, c * P:(c + 1) * P], w1_sb[:, :], start=True, stop=True)
                        ins.then_inc(pXe, 1)
                    if g:
                        dense_3(g)
                    if ph == 1:
                        wait(pe, aV, s.k + 1)
                        wait(pe, dS, seq(ph, s) + 1)
                        wait(pe, aU, seq(ph, s))
                        sum_equal(s, U)

                steps(pe, step, R, G)

            def product_y(b):
                wait(pe, a2e, b.k + 1)
                wait(pe, dRe, b.k)
                if b.is_any(0):
                    pe.wait_ge(dR, NG)
                for c in range(2):
                    for h, t in enumerate((x1Te, x2Te)):
                        ins = mm(bY[:, c * D:(c + 1) * D], t[:, c * P:(c + 1) * P], wo_sb[:, h, :],
                                 start=(h == 0), stop=(h == 1))
                ins.then_inc(pYe, 1)

            def sum_messages(b):
                wait(pe, aV, G + b.k + 1)
                wait(pe, dS, 2 * G + b.k + 1)
                wait(pe, aU, 2 * G + b.k)
                sum_equal(b, D)

            def step2(s):
                if not s.is_any(0):
                    product_y(s.at(-1))
                wait(pe, dAgg, G + s.k + 1)
                wait(pe, aTe, G + s.k)
                for c in range(2):
                    ins = nc.tensor.transpose(bE1[:, c * P:(c + 1) * P], agg[s.slot][:, c, :], ident[:, :])
                ins.then_inc(pTe, 1)
                wait(pe, aTe, G + s.k + 1)
                wait(pe, a2e, s.k)
                mm(bH[:, 0:2 * P], w1_sb[:, :], aggT[:, :], start=True, stop=True).then_inc(p1e, 1)
                wait(pe, a1e, s.k + 1)
                wait(pe, dS1, s.k)
                if s.is_any(0):
                    pe.wait_ge(dPre, G)
                for c in range(2):
                    ins = nc.tensor.transpose(bE2[:, c * D:(c + 1) * D], x1Te[:, c * P:(c + 1) * P], ident[:, :])
                ins.then_inc(pT2, 1)
                wait(pe, dS2, s.k + 1)
                wait(pe, aT3, s.k)
                for c in range(2):
                    ins = nc.tensor.transpose(bT[:, c * P:(c + 1) * P], s2[:, c, :], ident[:, :])
                ins.then_inc(pT3, 1)
                wait(pe, aT3, s.k + 1)
                mm(bH[:, 0:2 * P], w2_sb[:, :], s2T[:, :], start=True, stop=True).then_inc(p2e, 1)
                if not s.is_any(0):
                    sum_messages(s.at(-1))

            steps(pe, step2, R, G)
            product_y(edge(G - 1))
            sum_messages(edge(G - 1))

            def transpose_h(g):
                p, j = dims(g)
                wait(pe, oH, g.k + 1)
                wait(pe, oTc, g.k)
                for q in range(j):
                    ins = nc.tensor.transpose(bT[:, q * p:(q + 1) * p], ta[g.slot][0:p, q, :], ident[0:p, 0:p])
                ins.then_inc(oTp, 1)

            transpose_h(dense(0))

            def step3(g):
                p, j = dims(g)
                wait(pe, oTc, g.k + 1)
                wait(pe, oR1, g.k)
                mm(bH[:, 0:p * j], v1_sb[:, :], xT[:, 0:p * j], start=True, stop=True).then_inc(oM1, 1)
                if not g.is_any(NG - 1):
                    transpose_h(g.at(1))
                wait(pe, oR1, g.k + 1)
                wait(pe, oR, g.k)
                if g.is_any(0):
                    pe.wait_ge(dRe, G)
                for q in range(j):
                    ins = mm(bY[0:p, q * D:(q + 1) * D], x1T[:, q * p:(q + 1) * p], v2_sb[:, :], start=True, stop=True)
                ins.then_inc(oM2, 1)

            steps(pe, step3, RD, NG)


_INS = ["x", "src", "dst", "edge_attr_128", "L0_gnn_W1", "L0_gnn_b1", "L0_gnn_W2", "L0_gnn_b2", "L0_gnn_Wout",
        "L0_gnn_bout", "L1_gnn_W1", "L1_gnn_b1", "L1_gnn_W2", "L1_gnn_b2", "L1_gnn_eps"]


def kernel(**inputs):
    import numpy as _np
    import concourse.bacc as _bacc
    from concourse import mybir as _mybir
    from concourse.bass_utils import run_bass_kernel_spmd as _run

    nc = _bacc.Bacc("TRN2", target_bir_lowering=False, num_devices=1)
    arrays, args = {}, []
    for name in _INS:
        a = _np.ascontiguousarray(inputs[name])
        if a.ndim == 0:
            a = a.reshape(1)
        arrays[f"in_{name}"] = a
        args.append(nc.dram_tensor(f"in_{name}", a.shape, _mybir.dt.from_np(a.dtype), kind="ExternalInput").ap())
    shape = inputs["x"].shape
    out = nc.dram_tensor("out_0", shape, _mybir.dt.float32, kind="ExternalOutput").ap()
    gnn(nc, *args, out)
    r = _run(nc, [arrays], core_ids=[0])
    return r.results[0]["out_0"]
```

```python
import concourse.bass as bass
from concourse import mybir
from contextlib import ExitStack

F32 = mybir.dt.float32
I32 = mybir.dt.int32
ALU = mybir.AluOpType
ACT = mybir.ActivationFunctionType

R = 7
RD = 6


class At:

    def __init__(self, ring, i, off):
        self.ring, self.i, self.off = ring, i, off
        self.k = ring * i + off
        self.slot = off % ring
        self.lap = i + off // ring

    def at(self, d):
        return At(self.ring, self.i, self.off + d)

    def is_any(self, *ks):
        return isinstance(self.k, int) and self.k in ks

    def is_from(self, k):
        return isinstance(self.k, int) and self.k >= k


def edge(k):
    return At(R, 0, k)


def dense(k):
    return At(RD, 0, k)


def steps(body, eng, ring, count, drain):
    laps = (count - 2 * ring) // ring
    for k in range(ring):
        body(At(ring, 0, k))
    with eng.Fori(0, laps) as i:
        for u in range(ring):
            body(At(ring, i, ring + u))
    for k in range(ring * (laps + 1), count + drain):
        body(At(ring, 0, k))


def lagging(stage, s, lag, count):
    if not (isinstance(s.k, int) and not 0 <= s.k - lag < count):
        stage(s.at(-lag))


def wait(eng, sem, value):
    if not (isinstance(value, int) and value == 0):
        eng.wait_ge(sem, value)


def gnn(nc, x, src, dst, edge_attr, w1, b1, w2, b2, wout, bout, v1, c1, v2, c2, eps, out):
    N, D = x.shape
    E = src.shape[0]
    P = 128
    T = -(-E // P)
    G = T // 2
    assert T == 2 * G and G == R * R
    NG = -(-N // (4 * P))
    assert NG == 2 * G
    FULL = NG - 1
    LEFT = N - FULL * 4 * P
    LP, LJ = LEFT // 3, 3
    assert LP * LJ == LEFT and LP % 16 == 0
    ELEFT = E - (T - 1) * P
    NT = -(-(N + 3 * P) // P) * P
    U = D + 4
    L, LD = R - 1, RD - 1
    L2 = 4
    LAG1, LAG2, LAGD = 1, 3, 3
    MID = 2
    PRE = NG - 2 * RD * R - MID
    FJ = 4 * NG
    A0_CHUNKS, CHUNK = 14, FJ // G
    A0_CHUNK = FJ // A0_CHUNKS
    assert FJ == A0_CHUNK * A0_CHUNKS == CHUNK * G and N <= P * FJ <= NT
    LN_EPS = 1e-5

    C = nc.dram_tensor("sums_a0_a1", (NT, 2 * U), F32).ap()
    A2 = nc.dram_tensor("sums_a2", (NT, D), F32).ap()
    Y = nc.dram_tensor("table_y", (NT, D), F32).ap()
    SRCROWS = nc.dram_tensor("src_as_float", (T, P), F32).ap()
    DSTROWS = nc.dram_tensor("dst_as_float", (T, P), F32).ap()
    C_units = C.rearrange("n (s u) -> (n s) u", s=2)
    C_filled = C[0:P * FJ].rearrange("(p j) (s u) -> p j s u", p=P, s=2)
    C_rest = C[P * FJ:NT].rearrange("(j p) u -> p j u", p=P)
    A2_filled = A2[0:P * FJ].rearrange("(p j) d -> p j d", p=P)
    A2_rest = A2[P * FJ:NT].rearrange("(j p) d -> p j d", p=P)

    def rows4(t):
        return t[0:FULL * 4 * P].rearrange("(g p j) d -> g p j d", p=P, j=4)

    def rows3(t):
        return t[FULL * 4 * P:N].rearrange("(p j) d -> p j d", j=LJ)

    x4, y4, a24, out4 = rows4(x), rows4(Y), rows4(A2), rows4(out)
    x3, y3, a23, out3 = rows3(x), rows3(Y), rows3(A2), rows3(out)
    rb_src = SRCROWS.rearrange("(g c) p -> g (c p)", c=2)
    rb_dst = DSTROWS.rearrange("(g c) p -> g (c p)", c=2)
    ea2 = edge_attr[0:(T - 2) * P].rearrange("(g c p) d -> g p c d", c=2, p=P)

    ctx = ExitStack()
    with ctx:
        def sb(name, shape, dt=F32):
            return ctx.enter_context(nc.sbuf_tensor(name, shape, dt))

        def ring(name, shape, dt=F32, slots=R):
            return [sb(f"{name}{i}", shape, dt) for i in range(slots)]

        def bank(name):
            return ctx.enter_context(nc.psum_tensor(name, [P, 512], F32))

        def sem(name):
            return ctx.enter_context(nc.semaphore(name))

        def sems(name, slots=R):
            return [sem(f"{name}{i}") for i in range(slots)]

        ident = sb("ident", [P, P])
        zeros = sb("zeros", [P, 2 * U])
        earlier = sb("earlier", [P, 2, 2 * P])
        spare_i = sb("spare_i", [P, 2], I32)
        spare = sb("spare", [P, 2])
        w1_sb, w2_sb, v1_sb, v2_sb = (sb(n, [P, D]) for n in ("w1s", "w2s", "v1s", "v2s"))
        wo_sb = sb("wos", [P, 2, D])
        b1_col, b2_col, c1_col, eps_col, eps1_col, ln_col = (sb(n, [P, 1]) for n in ("b1c", "b2c", "c1c", "epc", "ep1", "lnc"))
        b1_row, bo_row, c2_row = (sb(n, [P, D]) for n in ("b1r", "bor", "c2r"))
        rows_i = [sb(f"rows_i{n}", [T, P], I32) for n in range(2)]
        rows_f = [sb(f"rows_f{n}", [T, P]) for n in range(2)]
        raw = [sb(f"raw{n}", [P, T]) for n in range(2)]
        off_spare = [sb(f"offs{n}", [P, G, 2]) for n in range(2)]
        near = [sb(f"near{n}", [P, T]) for n in range(2)]
        src_i, dst_i = (sb(n, [P, T], I32) for n in ("src_i", "dst_i"))
        both_i = sb("both_i", [P, G, 4], I32)
        to_a1 = sb("to_a1", [P, T], I32)
        to_y = sb("to_y", [P, T], I32)
        V = ring("V", [P, 2, U])
        UU = ring("U", [P, 2, U])
        S = ring("S", [P, 2, 2 * P])
        rb = ring("rb", [P, 2 * P])
        cs = ring("cs", [P, 2, 2 * U])
        ea = ring("ea", [P, 2, D])
        ye = ring("ye", [P, 2, D])
        agg = ring("agg", [P, 2, D])
        gi = ring("gi", [P, 4], I32)
        si = ring("si", [P, 2], I32)
        yi = ring("yi", [P, 2], I32)
        xkeep = sb("xkeep", [P, G, 2, D])
        aggT, s2T, x2Te = (sb(n, [P, 2 * P]) for n in ("aggT", "s2T", "x2Te"))
        x1Te = ring("x1Te", [P, 2 * P])
        pre, s1, s2, re, xbe = (sb(n, [P, 2, D]) for n in ("pre", "s1", "s2", "re", "xbe"))
        count, masked, row1 = (sb(n, [P, 2]) for n in ("count", "masked", "row1"))
        junk = sb("junk", [P, 2, 2 * P])
        deg, inv = (ring(n, [P, 2, 1]) for n in ("deg", "inv"))
        ste, mve = sb("ste", [P, 2, 6]), ring("mve", [P, 2, 2])
        sde, rse = (ring(n, [P, 2]) for n in ("sde", "rse"))
        xt = ring("xt", [P, 4, D], slots=RD)
        yd = ring("yd", [P, 4, D], slots=RD)
        ta = [c[:, :, :].rearrange("p c u -> p (c u)")[:, 0:4 * D].rearrange("p (j d) -> p j d", j=4) for c in cs[0:RD]]
        xT, x2T = (sb(n, [P, 4 * P]) for n in ("xT", "x2T"))
        x1T = ring("x1T", [P, 4 * P], slots=2)
        st = sb("st", [P, 4, 6])
        mv = ring("mv", [P, 4, 2], slots=RD)
        sd, rs, nm = (ring(n, [P, 4], slots=RD) for n in ("sd", "rs", "nm"))
        bT, bH1, bH2, bY, bE1, bE2, bU = (bank(n) for n in ("bT", "bH1", "bH2", "bY", "bE1", "bE2", "bU"))

        rb_in, gathered, kept, added, y_put, ea_in = (
            sems(n) for n in ("rb_in", "gathered", "kept", "added", "y_put", "ea_in"))
        xt_in, y_out = (sems(n, RD) for n in ("xt_in", "y_out"))
        w_in, idx_in, rows_out, fill_a0, fill_a1, fill_a2 = (
            sem(n) for n in ("w_in", "idx_in", "rows_out", "fill_a0", "fill_a1", "fill_a2"))
        (pool_c, pool_id, spare_ok, rows_ok, dve_c, rowsT, idx_ok, gi_ok, yi_ok, zeros_ok,
         v_ok, ln_ok) = (sem(n) for n in ("pool_c", "pool_id", "spare_ok", "rows_ok", "dve_c", "rowsT", "idx_ok",
                                          "gi_ok", "yi_ok", "zeros_ok", "v_ok", "ln_ok"))
        (pT, p1, p2, pY, aT, a1, a2, aS, aN, dX, dR, dSt, dMv, dRs, dNm) = (sem(n) for n in (
            "pT", "p1", "p2", "pY", "aT", "a1", "a2", "aS", "aN", "dX", "dR", "dSt", "dMv", "dRs", "dNm"))
        (dS, dCount, dMask, dRow, dSi, pU, aU) = (sem(n) for n in (
            "dS", "dCount", "dMask", "dRow", "dSi", "pU", "aU"))
        (dDeg, dInv, dAgg, pTe, aTe, pXe, dPre, aV) = (sem(n) for n in (
            "dDeg", "dInv", "dAgg", "pTe", "aTe", "pXe", "dPre", "aV"))
        (p1e, a1e, pT2, dS1, aS2, pT3, aT3, p2e, a2e, pYe, dXe, dRe, dSte, dMve, aSe, dRse, dNe, dM) = (sem(n) for n in (
            "p1e", "a1e", "pT2", "dS1", "aS2", "pT3", "aT3", "p2e", "a2e", "pYe", "dXe", "dRe", "dSte", "dMve", "aSe",
            "dRse", "dNe", "dM"))
        (oH, oTp, oTc, oM1, oR1, oM2, oB, oR, oSt, oMv, oSd, oRs, oNm, oN) = (sem(n) for n in (
            "oH", "oTp", "oTc", "oM1", "oR1", "oM2", "oB", "oR", "oSt", "oMv", "oSd", "oRs", "oNm", "oN"))

        waited = sem("waited")
        W_LOADS = 12
        block = ctx.enter_context(nc.Block())

        def dims(g):
            return (LP, LJ) if g.is_any(NG - 1) else (P, 4)

        def groups_in(slot):
            return len(range(slot, NG, RD))

        def seq(ph, s):
            return G * ph + s.k

        def dense_of(ph, s):
            if s.slot >= RD or s.is_from(G):
                return None
            return At(RD, s.i, PRE + (RD * R + MID) * ph + RD * (s.off // R) + s.slot)

        def stand_alone(eng):
            eng.sem_inc(waited, 1)

        @block.sync
        def _(sp):
            sp.wait_ge(rows_ok, 2)
            for n, idx in enumerate((src, dst)):
                sp.dma_start(rows_i[n][0:T - 1, :], idx[0:(T - 1) * P].rearrange("(t p) -> t p", p=P)).then_inc(idx_in, 16)
                sp.dma_start(rows_i[n][T - 1:T, 0:ELEFT],
                             idx[(T - 1) * P:E].rearrange("(t p) -> t p", t=1)).then_inc(idx_in, 16)
            for dest, source in ((w1_sb[:, :], w1), (w2_sb[:, :], w2), (v1_sb[:, :], v1), (v2_sb[:, :], v2),
                                 (wo_sb[:, :, :], wout.rearrange("(h p) d -> p h d", h=2)),
                                 (b1_col[:, :], b1.rearrange("(p o) -> p o", o=1)),
                                 (b2_col[:, :], b2.rearrange("(p o) -> p o", o=1)),
                                 (c1_col[:, :], c1.rearrange("(p o) -> p o", o=1)),
                                 (b1_row[:, :], b1.partition_broadcast(P)),
                                 (bo_row[:, :], bout.partition_broadcast(P)),
                                 (c2_row[:, :], c2.partition_broadcast(P)),
                                 (eps_col[:, :], eps.partition_broadcast(P))):
                sp.dma_start(dest, source).then_inc(w_in, 16)

            def load_x(g):
                if g.is_any(NG - 1):
                    sp.dma_start(xt[g.slot][0:LP, 0:LJ, :], x3).then_inc(xt_in[g.slot], 16)
                else:
                    sp.dma_start(xt[g.slot][:, :, :], x4[g.k]).then_inc(xt_in[g.slot], 16)

            def store_y(g):
                wait(sp, aN, g.k + 1)
                if g.is_any(NG - 1):
                    sp.dma_start(y3, yd[g.slot][0:LP, 0:LJ, :]).then_inc(y_out[g.slot], 16)
                else:
                    sp.dma_start(y4[g.k], yd[g.slot][:, :, :]).then_inc(y_out[g.slot], 16)

            def next_x(g):
                wait(sp, dR, g.k - LD)
                load_x(g)

            def dense_step(g):
                if not g.is_any(0):
                    lagging(next_x, g, 1 - LD, NG)
                lagging(store_y, g, 3, NG)

            for k in range(LD):
                load_x(dense(k))
            sp.wait_ge(dve_c, 2)
            sp.dma_start(SRCROWS, rows_f[0][:, :]).then_inc(rows_out, 16)
            sp.dma_start(DSTROWS, rows_f[1][:, :]).then_inc(rows_out, 16)

            sp.wait_ge(zeros_ok, 1)
            sp.dma_start(C_rest, zeros[:, 0:2 * U].unsqueeze(1).broadcast_to([P, NT // P - FJ, 2 * U])).then_inc(fill_a0, 16)
            for k in range(A0_CHUNKS):
                sp.dma_start(C_filled[:, A0_CHUNK * k:A0_CHUNK * (k + 1), 0, :],
                             zeros[:, 0:U].unsqueeze(1).broadcast_to([P, A0_CHUNK, U])).then_inc(fill_a0, 16)
                if k < PRE:
                    dense_step(dense(k))
            sp.dma_start(A2_rest, zeros[:, 0:D].unsqueeze(1).broadcast_to([P, NT // P - FJ, D])).then_inc(fill_a2, 16)
            sp.wait_ge(rows_out, 32)

            def load_rb(ph, d):
                table = rb_dst if ph == 2 else rb_src
                sp.dma_start(rb[d.slot][:, :], table[d.k].partition_broadcast(P)).then_inc(rb_in[d.slot], 16)

            def zeros_a1(s):
                sp.dma_start(C_filled[:, bass.ds(CHUNK * s.k, CHUNK), 1, :],
                             zeros[:, 0:U].unsqueeze(1).broadcast_to([P, CHUNK, U])).then_inc(fill_a1, 16)

            def zeros_a2(s):
                sp.dma_start(A2_filled[:, bass.ds(CHUNK * s.k, CHUNK), :],
                             zeros[:, 0:D].unsqueeze(1).broadcast_to([P, CHUNK, D])).then_inc(fill_a2, 16)

            def keep_x(ph, d):
                if ph == 0:
                    wait(sp, gathered[d.slot], 32 * (d.lap + 1))
                    rows = V[d.slot][:, :, 0:D]
                else:
                    wait(sp, gathered[d.slot], 32 * R + 64 * (d.lap + 1))
                    stand_alone(sp)
                    wait(sp, dAgg, d.k + 1)
                    rows = cs[d.slot][:, :, U:U + D]
                stand_alone(sp)
                sp.dma_start(xkeep[:, bass.ds(d.k, 1), :, :].rearrange("p a c d -> p (a c) d"), rows).then_inc(kept[d.slot], 16)

            for ph in range(2):
                wait(sp, dS, G * ph)
                for k in range(L):
                    load_rb(ph, edge(k))
                if ph == 1:
                    for k in range(MID):
                        dense_step(dense(PRE + RD * R + k))

                def next_rb(d, ph=ph):
                    wait(sp, dS, seq(ph, d) - L)
                    load_rb(ph, d)

                def step(s, ph=ph):
                    lagging(next_rb, s, -L, G)
                    if g := dense_of(ph, s):
                        dense_step(g)
                    lagging((zeros_a1, zeros_a2)[ph], s, 0, G)
                    lagging(lambda d: keep_x(ph, d), s, 0, G)

                steps(step, sp, R, G, ph * LAG1)
            for k in range(NG, NG + LAGD):
                dense_step(dense(k))

            def load_ea(d):
                if d.is_any(G - 1):
                    sp.dma_start(ea[d.slot][:, 0, :], edge_attr[(T - 2) * P:(T - 1) * P]).then_inc(ea_in[d.slot], 16)
                    sp.dma_start(ea[d.slot][0:ELEFT, 1, :], edge_attr[(T - 1) * P:E]).then_inc(ea_in[d.slot], 16)
                else:
                    sp.dma_start(ea[d.slot][:, :, :], ea2[d.k]).then_inc(ea_in[d.slot], 16)

            sp.wait_ge(dS, 2 * G)
            for k in range(L):
                load_rb(2, edge(k))
            for k in range(LAG2):
                load_ea(edge(k))

            def next_rb(d):
                wait(sp, dS, seq(2, d) - L)
                load_rb(2, d)

            def next_ea(d):
                if not d.is_any(*range(R)):
                    wait(sp, dM, d.k - R + 1)
                load_ea(d)

            def step2(s):
                lagging(next_rb, s, -L, G)
                lagging(next_ea, s, -LAG2, G)

            steps(step2, sp, R, G, LAG2)

            for n in range(R):
                sp.wait_ge(y_put[n], 32 * R)
                sp.wait_ge(added[n], 32 * 3 * R)

            def load_ya(g):
                if g.is_any(NG - 1):
                    sp.dma_start(xt[g.slot][0:LP, 0:LJ, :], y3).then_inc(xt_in[g.slot], 16)
                    sp.dma_start(ta[g.slot][0:LP, 0:LJ, :], a23).then_inc(xt_in[g.slot], 16)
                else:
                    sp.dma_start(xt[g.slot][:, :, :], y4[g.k]).then_inc(xt_in[g.slot], 16)
                    sp.dma_start(ta[g.slot][:, :, :], a24[g.k]).then_inc(xt_in[g.slot], 16)

            def store_out(g):
                wait(sp, oN, g.k + 1)
                if g.is_any(NG - 1):
                    sp.dma_start(out3, yd[g.slot][0:LP, 0:LJ, :]).then_inc(y_out[g.slot], 16)
                else:
                    sp.dma_start(out4[g.k], yd[g.slot][:, :, :]).then_inc(y_out[g.slot], 16)

            for k in range(LD):
                load_ya(dense(k))

            def next_ya(g):
                wait(sp, oTp, g.k - LD)
                wait(sp, oR, g.k - LD)
                load_ya(g)

            def step3(g):
                if not g.is_any(0):
                    lagging(next_ya, g, 1 - LD, NG)
                lagging(store_out, g, 3, NG)

            steps(step3, sp, RD, NG, LAGD)
            for n in range(RD):
                sp.wait_ge(y_out[n], 16 * 2 * groups_in(n))

        @block.gpsimd
        def _(pool):
            for n in range(2):
                nc.gpsimd.iota(rows_i[n][:, :], [[1, P]], base=N + 2 * P, channel_multiplier=0).then_inc(rows_ok, 1)
            nc.gpsimd.memset(ident[:, :], 0.0).then_inc(pool_c, 1)
            nc.gpsimd.memset(earlier[:, :, :], 1.0).then_inc(pool_c, 1)
            nc.gpsimd.iota(spare_i[:, :], [[P, 2]], base=N, channel_multiplier=1).then_inc(spare_ok, 1)
            pool.wait_ge(pool_c, 2)
            nc.gpsimd.affine_select(out=ident[:, :], in_=ident[:, :], compare_op=ALU.not_equal, fill=1.0, base=0,
                                    pattern=[[-1, P]], channel_multiplier=1).then_inc(pool_id, 1)
            nc.gpsimd.affine_select(out=earlier[:, :, :], in_=earlier[:, :, :], compare_op=ALU.is_gt, fill=0.0, base=0,
                                    pattern=[[P, 2], [-1, 2 * P]], channel_multiplier=1).then_inc(pool_id, 1)

            def copy_gi(ph, d):
                wait(pool, gathered[d.slot], (0, 32 * R, 96 * R)[ph] + (32, 64, 32)[ph] * d.lap)
                if ph == 1:
                    ins = nc.gpsimd.tensor_copy(gi[d.slot][:, :], both_i[:, bass.ds(d.k, 1), :].rearrange("p a c -> p (a c)"))
                else:
                    ins = nc.gpsimd.tensor_copy(gi[d.slot][:, 0:2], (dst_i, None, src_i)[ph][:, bass.ds(2 * d.k, 2)])
                ins.then_inc(gi_ok, 1)

            def rows_of(index, c):
                return bass.IndirectOffsetOnAxis(ap=index[:, c:c + 1], axis=0)

            def gather(ph, d):
                wait(pool, gi_ok, seq(ph, d) + 1)
                stand_alone(pool)
                for c in range(2):
                    if ph == 0:
                        pool.indirect_dma_start(out=V[d.slot][:, c, 0:D], out_offset=None, in_=x,
                                                in_offset=rows_of(gi[d.slot], c)).then_inc(gathered[d.slot], 16)
                    elif ph == 1:
                        pool.indirect_dma_start(out=cs[d.slot][:, c, 0:U], out_offset=None, in_=C_units,
                                                in_offset=rows_of(gi[d.slot], c)).then_inc(gathered[d.slot], 16)
                        pool.indirect_dma_start(out=cs[d.slot][:, c, U:U + D], out_offset=None, in_=x,
                                                in_offset=rows_of(gi[d.slot], 2 + c)).then_inc(gathered[d.slot], 16)
                    else:
                        pool.indirect_dma_start(out=cs[d.slot][:, c, :], out_offset=None, in_=C,
                                                in_offset=rows_of(gi[d.slot], c)).then_inc(gathered[d.slot], 16)

            def add_rows(ph, s, index):
                wait(pool, aU, seq(ph, s) + 1)
                if not (ph == 0 and s.is_any(0)):
                    b = s.at(-1)
                    wait(pool, added[b.slot], 32 * (R * ph + b.lap + 1))
                stand_alone(pool)
                for c in range(2):
                    pool.indirect_dma_start(out=A2 if ph == 2 else C_units, out_offset=rows_of(index, c),
                                            in_=UU[s.slot][:, c, 0:D] if ph == 2 else UU[s.slot][:, c, :], in_offset=None,
                                            compute_op=ALU.add).then_inc(added[s.slot], 16)

            pool.wait_ge(idx_ok, 2)
            pool.wait_ge(v_ok, 1)
            for ph in range(2):
                if ph == 1:
                    pool.wait_ge(added[(G - 1) % R], 32 * R)
                copy_gi(ph, edge(0))
                for k in range(L):
                    gather(ph, edge(k))
                    copy_gi(ph, edge(k + 1))
                if ph == 0:
                    pool.wait_ge(fill_a0, 16 * (A0_CHUNKS + 1))
                else:
                    pool.wait_ge(fill_a1, 16 * G)

                def next_gather(d, ph=ph):
                    if ph == 0:
                        wait(pool, pU, d.k - L)
                        wait(pool, kept[d.slot], 16 * d.lap)
                    else:
                        wait(pool, dAgg, d.k - L)
                        wait(pool, kept[d.slot], 16 * (R + d.lap))
                    gather(ph, d)

                def scatter(b, ph=ph):
                    if ph == 1:
                        nc.gpsimd.tensor_copy(si[b.slot][:, :], to_a1[:, bass.ds(2 * b.k, 2)]).then_inc(yi_ok, 1)
                        wait(pool, yi_ok, b.k + 1)
                    else:
                        wait(pool, dSi, b.k + 1)
                    add_rows(ph, b, si[b.slot])

                def step(s, ph=ph):
                    lagging(next_gather, s, -L, G)
                    lagging(lambda d: copy_gi(ph, d), s, -L - 1, G)
                    lagging(scatter, s, ph * LAG1, G)

                steps(step, pool, R, G, ph * LAG1)

            pool.wait_ge(added[(G - 1) % R], 32 * 2 * R)
            for n in range(R):
                pool.wait_ge(kept[n], 16 * 2 * R)
            copy_gi(2, edge(0))
            for k in range(L2):
                gather(2, edge(k))
                copy_gi(2, edge(k + 1))
            pool.wait_ge(fill_a2, 16 * (G + 1))
            for n in range(RD):
                pool.wait_ge(y_out[n], 16 * groups_in(n))

            def put(b):
                nc.gpsimd.tensor_copy(yi[b.slot][:, :], to_y[:, bass.ds(2 * b.k, 2)]).then_inc(yi_ok, 1)
                wait(pool, dNe, b.k + 1)
                wait(pool, yi_ok, G + b.k + 1)
                if not b.is_any(0):
                    a = b.at(-1)
                    wait(pool, y_put[a.slot], 32 * (a.lap + 1))
                stand_alone(pool)
                for c in range(2):
                    pool.indirect_dma_start(out=Y, out_offset=rows_of(yi[b.slot], c), in_=ye[b.slot][:, c, :],
                                            in_offset=None).then_inc(y_put[b.slot], 16)
                wait(pool, dSi, G + b.k + 1)
                add_rows(2, b, si[b.slot])

            def next_gather2(d):
                if not d.is_any(*range(R)):
                    wait(pool, dS1, d.k - R + 1)
                gather(2, d)

            def step2(s):
                lagging(next_gather2, s, -L2, G)
                lagging(lambda d: copy_gi(2, d), s, -L2 - 1, G)
                lagging(put, s, LAG2, G)

            steps(step2, pool, R, G, LAG2)

            def step3(g):
                p, j = dims(g)
                wait(pool, oH, g.k + 1)
                nc.gpsimd.tensor_tensor(xt[g.slot][0:p, 0:j, :], xt[g.slot][0:p, 0:j, :],
                                        c2_row[0:p, :].unsqueeze(1).broadcast_to([p, j, D]), ALU.add).then_inc(oB, 1)

            steps(step3, pool, RD, NG, 0)

        @block.scalar
        def _(act):
            def copy_xT(g):
                p, j = dims(g)
                wait(act, pT, g.k + 1)
                wait(act, p1, g.k)
                nc.scalar.activation(xT[:, 0:p * j], bT[:, 0:p * j], ACT.Copy).then_inc(aT, 1)

            def root(g, moments, done):
                wait(act, moments, g.k + 1)
                p, j = dims(g)
                nc.scalar.activation(sd[g.slot][0:p, 0:j], mv[g.slot][0:p, 0:j, 1], ACT.Sqrt,
                                     bias=ln_col[0:p, :]).then_inc(done, 1)

            def scale(g, ready, done):
                p, j = dims(g)
                wait(act, ready, g.k + 1)
                for q in range(j):
                    ins = nc.scalar.activation(yd[g.slot][0:p, q, :], yd[g.slot][0:p, q, :], ACT.Identity,
                                               scale=rs[g.slot][0:p, q:q + 1], bias=nm[g.slot][0:p, q:q + 1])
                ins.then_inc(done, 1)

            def relu_1(g):
                p, j = dims(g)
                wait(act, p1, g.k + 1)
                if not g.is_any(0, 1):
                    wait(act, pY, g.k - 1)
                nc.scalar.activation(x1T[g.slot % 2][:, 0:p * j], bH1[:, 0:p * j], ACT.Relu, bias=b1_col[:, :]).then_inc(a1, 1)

            def relu_2(g):
                p, j = dims(g)
                wait(act, p2, g.k + 1)
                wait(act, pY, g.k)
                nc.scalar.activation(x2T[:, 0:p * j], bH2[:, 0:p * j], ACT.Relu, bias=b2_col[:, :]).then_inc(a2, 1)

            def dense_1(g):
                lagging(relu_1, g, 0, NG)

            def dense_2(g):
                lagging(relu_2, g, 0, NG)
                lagging(copy_xT, g, -1, NG)

            def dense_3(g):
                lagging(lambda b: root(b, dMv, aS), g, 2, NG)
                lagging(lambda b: scale(b, dNm, aN), g, 3, NG)

            def dense_step(g):
                dense_1(g)
                dense_2(g)
                dense_3(g)

            act.wait_ge(w_in, 16 * W_LOADS)
            act.wait_ge(ln_ok, 1)
            copy_xT(dense(0))
            for k in range(PRE):
                dense_step(dense(k))

            def copy_aggT(ph, s):
                n = seq(ph - 1, s)
                wait(act, pTe, n + 1)
                if ph == 1:
                    wait(act, pXe, s.k)
                else:
                    wait(act, p1e, s.k)
                nc.scalar.activation(aggT[:, :], bE1[:, 0:2 * P], ACT.Copy).then_inc(aTe, 1)

            def relu_v(ph, s):
                wait(act, (None, dPre, dM)[ph], s.k + 1)
                nc.scalar.activation(V[s.slot][:, :, 0:D], pre[:, :, :], ACT.Relu).then_inc(aV, 1)

            def copy_sums(ph, s):
                wait(act, pU, seq(ph, s) + 1)
                wait(act, added[s.slot], 32 * (R * ph + s.lap))
                w = D if ph == 2 else U
                nc.scalar.activation(UU[s.slot][:, :, 0:w], bU[:, 0:2 * w].rearrange("p (c u) -> p c u", c=2),
                                     ACT.Copy).then_inc(aU, 1)

            for ph in range(2):
                def step(s, ph=ph):
                    g = dense_of(ph, s)
                    if g:
                        dense_1(g)
                    if ph == 1:
                        lagging(lambda b: relu_v(1, b), s, 1, G)
                        lagging(lambda b: copy_aggT(1, b), s, 0, G)
                    if g:
                        dense_2(g)
                    lagging(lambda b: copy_sums(ph, b), s, ph * LAG1, G)
                    if g:
                        dense_3(g)

                if ph == 1:
                    for k in range(MID):
                        dense_step(dense(PRE + RD * R + k))
                steps(step, act, R, G, ph * LAG1)
            for k in range(NG, NG + LAGD):
                dense_step(dense(k))

            def relu_1e(s):
                wait(act, p1e, s.k + 1)
                if not s.is_any(*range(R)):
                    wait(act, pYe, s.k - R + 1)
                nc.scalar.activation(x1Te[s.slot][:, :], bH1[:, 0:2 * P], ACT.Relu, bias=b1_col[:, :]).then_inc(a1e, 1)

            def scale_s(s):
                wait(act, dS1, s.k + 1)
                wait(act, pT3, s.k)
                for c in range(2):
                    ins = nc.scalar.activation(s2[:, c, :], s1[:, c, :], ACT.Copy, scale=inv[s.slot][:, c, :])
                ins.then_inc(aS2, 1)

            def copy_s2T(s):
                wait(act, pT3, s.k + 1)
                wait(act, p2e, s.k)
                nc.scalar.activation(s2T[:, :], bT[:, 0:2 * P], ACT.Copy).then_inc(aT3, 1)

            def relu_2e(s):
                wait(act, p2e, s.k + 1)
                wait(act, pYe, s.k)
                nc.scalar.activation(x2Te[:, :], bH2[:, 0:2 * P], ACT.Relu, bias=b2_col[:, :]).then_inc(a2e, 1)

            def root_e(b):
                wait(act, dMve, b.k + 1)
                nc.scalar.activation(sde[b.slot][:, :], mve[b.slot][:, :, 1], ACT.Sqrt, bias=ln_col[:, :]).then_inc(aSe, 1)

            def step2(s):
                lagging(lambda b: copy_aggT(2, b), s, 0, G)
                lagging(scale_s, s, 1, G)
                lagging(lambda b: relu_v(2, b), s, 3, G)
                lagging(copy_s2T, s, 1, G)
                lagging(relu_1e, s, 0, G)
                lagging(lambda b: copy_sums(2, b), s, 3, G)
                lagging(relu_2e, s, 1, G)
                lagging(root_e, s, 2, G)

            steps(step2, act, R, G, LAG2)

            def copy_hT(g):
                p, j = dims(g)
                wait(act, oTp, g.k + 1)
                wait(act, oM1, g.k)
                nc.scalar.activation(xT[:, 0:p * j], bT[:, 0:p * j], ACT.Copy).then_inc(oTc, 1)

            copy_hT(dense(0))

            def relu_3(g):
                p, j = dims(g)
                wait(act, oM1, g.k + 1)
                if not g.is_any(0, 1):
                    wait(act, oM2, g.k - 1)
                nc.scalar.activation(x1T[g.slot % 2][:, 0:p * j], bH1[:, 0:p * j], ACT.Relu, bias=c1_col[:, :]).then_inc(oR1, 1)

            def step3(g):
                lagging(relu_3, g, 0, NG)
                lagging(copy_hT, g, -1, NG)
                lagging(lambda b: root(b, oMv, oSd), g, 2, NG)
                lagging(lambda b: scale(b, oNm, oN), g, 3, NG)

            steps(step3, act, RD, NG, LAGD)

        @block.vector
        def _(dve):
            v = nc.vector
            v.memset(zeros[:, :], 0.0).then_inc(zeros_ok, 1)
            v.memset(ln_col[:, :], LN_EPS).then_inc(ln_ok, 1)
            for n in range(R):
                ins = v.memset(V[n][:, :, D:U], 1.0)
            ins.then_inc(v_ok, 1)
            dve.wait_ge(idx_in, 64)
            for n in range(2):
                v.tensor_copy(rows_f[n][:, :], rows_i[n][:, :]).then_inc(dve_c, 1)
            dve.wait_ge(spare_ok, 1)
            v.tensor_copy(spare[:, :], spare_i[:, :]).then_inc(dve_c, 1)
            dve.wait_ge(rowsT, 1)
            for n, b in enumerate((bE1, bE2)):
                v.tensor_copy(raw[n][:, :], b[:, 0:T]).then_inc(dve_c, 1)
            dve.wait_ge(dve_c, 5)
            for n in range(2):
                v.tensor_scalar(near[n][:, :], raw[n][:, :], float(N - 1), None, ALU.min).then_inc(dve_c, 1)
                v.tensor_tensor(off_spare[n][:, :, :], raw[n][:, :].rearrange("p (g c) -> p g c", c=2),
                                spare[:, :].unsqueeze(1).broadcast_to([P, G, 2]), ALU.subtract).then_inc(dve_c, 1)
            dve.wait_ge(dve_c, 9)
            v.tensor_copy(src_i[:, :], near[0][:, :])
            v.tensor_scalar(both_i[:, :, 0:2], near[1][:, :].rearrange("p (g c) -> p g c", c=2), 2.0, None, ALU.mult)
            v.tensor_copy(both_i[:, :, 2:4], near[0][:, :].rearrange("p (g c) -> p g c", c=2))
            v.tensor_copy(dst_i[:, :], near[1][:, :]).then_inc(idx_ok, 1)
            dve.wait_ge(w_in, 16 * W_LOADS)
            v.tensor_scalar(eps1_col[:, :], eps_col[:, :], 1.0, None, ALU.add).then_inc(idx_ok, 1)

            def residual(g, product, other, stored, summed):
                p, j = dims(g)
                wait(dve, product, g.k + 1)
                wait(dve, other, g.k + 1)
                wait(dve, y_out[g.slot], 16 * ((groups_in(g.slot) if stored else 0) + g.lap))
                v.tensor_tensor(yd[g.slot][0:p, 0:j, :], bY[0:p, 0:j * D].rearrange("p (j d) -> p j d", j=j),
                                xt[g.slot][0:p, 0:j, :], ALU.add).then_inc(summed, 1)

            def statistics(g, summed, stats, done):
                p, j = dims(g)
                wait(dve, summed, g.k + 1)
                wait(dve, done, g.k)
                for q in range(j):
                    ins = v.bn_stats(st[0:p, q, :], yd[g.slot][0:p, q, :])
                ins.then_inc(stats, 1)

            def moments(g, stats, done):
                p, j = dims(g)
                wait(dve, stats, g.k + 1)
                stand_alone(dve)
                for q in range(j):
                    ins = v.bn_aggr(mv[g.slot][0:p, q, :], st[0:p, q, :])
                ins.then_inc(done, 1)

            def inverse(g, rooted, inverted):
                p, j = dims(g)
                wait(dve, rooted, g.k + 1)
                v.reciprocal(rs[g.slot][0:p, 0:j], sd[g.slot][0:p, 0:j]).then_inc(inverted, 1)

            def shift(g, inverted, done):
                p, j = dims(g)
                wait(dve, inverted, g.k + 1)
                v.scalar_tensor_tensor(out=nm[g.slot][0:p, 0:j], in0=mv[g.slot][0:p, 0:j, 0], scalar=-1.0,
                                       in1=rs[g.slot][0:p, 0:j], op0=ALU.mult, op1=ALU.mult).then_inc(done, 1)

            def add_bout(g):
                p, j = dims(g)
                wait(dve, pT, g.k + 1)
                v.tensor_tensor(xt[g.slot][0:p, 0:j, :], xt[g.slot][0:p, 0:j, :],
                                bo_row[0:p, :].unsqueeze(1).broadcast_to([p, j, D]), ALU.add).then_inc(dX, 1)

            def dense_1(g):
                lagging(add_bout, g, 0, NG)

            def dense_2(g):
                lagging(lambda b: residual(b, pY, dX, False, dR), g, 1, NG)

            def dense_3(g):
                lagging(lambda b: inverse(b, aS, dRs), g, 2, NG)
                lagging(lambda b: statistics(b, dR, dSt, dMv), g, 1, NG)

            def dense_4(g):
                lagging(lambda b: shift(b, dRs, dNm), g, 2, NG)
                lagging(lambda b: moments(b, dSt, dMv), g, 1, NG)

            def dense_step(g):
                dense_1(g)
                dense_2(g)
                dense_3(g)
                dense_4(g)

            def equal(ph, d, presums):
                which = 1 if ph == 2 else 0
                wait(dve, rb_in[d.slot], 16 * (R * ph + d.lap + 1))
                wait(dve, pU, presums)
                for c in range(2):
                    ins = v.tensor_scalar(S[d.slot][:, c, :], rb[d.slot][:, :], raw[which][:, bass.ds(2 * d.k + c, 1)], None,
                                          ALU.is_equal)
                ins.then_inc(dS, 1)

            def nth(ph, d):
                return (G if ph == 2 else 0) + d.k + 1

            def count_earlier(ph, d):
                wait(dve, dS, G * ph + d.k + 1)
                wait(dve, dSi, nth(ph, d) - 1)
                for c in range(2):
                    ins = v.tensor_tensor_reduce(out=junk[:, c, :], in0=S[d.slot][:, c, :], in1=earlier[:, c, :], scale=1.0,
                                                 scalar=0.0, op0=ALU.mult, op1=ALU.add, accum_out=count[:, c:c + 1])
                ins.then_inc(dCount, 1)

            def mask_rows(ph, d):
                which = 1 if ph == 2 else 0
                wait(dve, dCount, nth(ph, d))
                v.scalar_tensor_tensor(out=masked[:, :], in0=count[:, :], scalar=0.0,
                                       in1=off_spare[which][:, bass.ds(d.k, 1), :].rearrange("p a c -> p (a c)"),
                                       op0=ALU.is_equal, op1=ALU.mult).then_inc(dMask, 1)

            def add_spare(ph, d):
                wait(dve, dMask, nth(ph, d))
                v.tensor_tensor(row1[:, :], masked[:, :], spare[:, :], ALU.add).then_inc(dRow, 1)

            def write_rows(ph, d):
                wait(dve, dRow, nth(ph, d))
                wait(dve, added[d.slot], 32 * (R * ph + d.lap))
                if ph == 0:
                    v.tensor_scalar(to_a1[:, bass.ds(2 * d.k, 2)], row1[:, :], 2.0, 1.0, ALU.mult, ALU.add)
                    v.tensor_copy(to_y[:, bass.ds(2 * d.k, 2)], row1[:, :])
                v.tensor_scalar(si[d.slot][:, :], row1[:, :], 2.0 if ph == 0 else 1.0, None, ALU.mult).then_inc(dSi, 1)

            def kept_x(d):
                return xkeep[:, bass.ds(d.k, 1), :, :].rearrange("p a c d -> p (a c) d")

            def all_kept(ph):
                for n in range(R):
                    dve.wait_ge(kept[n], 16 * R * ph)

            def add_a0(ph, d):
                if ph == 1:
                    wait(dve, gathered[d.slot], 32 * R + 64 * (d.lap + 1))
                else:
                    wait(dve, gathered[d.slot], 96 * R + 32 * (d.lap + 1))
                v.tensor_tensor(agg[d.slot][:, :, :], kept_x(d), cs[d.slot][:, :, 0:D], ALU.add)
                v.tensor_scalar(deg[d.slot][:, :, :], cs[d.slot][:, :, D:D + 1], 1.0, 1.0, ALU.add, ALU.max).then_inc(dDeg, 1)

            def invert_degree(ph, d):
                wait(dve, dDeg, seq(ph - 1, d) + 1)
                v.reciprocal(inv[d.slot][:, :, :], deg[d.slot][:, :, :]).then_inc(dInv, 1)

            def mean(ph, d):
                wait(dve, dInv, seq(ph - 1, d) + 1)
                v.tensor_tensor(agg[d.slot][:, :, :], agg[d.slot][:, :, :], inv[d.slot][:, :, :].broadcast_to([P, 2, D]),
                                ALU.mult).then_inc(dAgg, 1)

            def add_b1(s):
                wait(dve, pXe, s.k + 1)
                wait(dve, aV, s.k)
                v.tensor_tensor(pre[:, :, :], bE2[:, 0:2 * D].rearrange("p (c d) -> p c d", c=2),
                                b1_row[:, :].unsqueeze(1).broadcast_to([P, 2, D]), ALU.add).then_inc(dPre, 1)

            for k in range(PRE):
                dense_step(dense(k))

            for ph in range(2):
                presums = G * ph
                equal(ph, edge(0), presums)
                if ph == 0:
                    for f in (count_earlier, mask_rows, add_spare, write_rows):
                        f(0, edge(0))
                else:
                    for k in range(MID):
                        dense_step(dense(PRE + RD * R + k))
                    all_kept(1)
                    for f in (add_a0, invert_degree, mean):
                        f(1, edge(0))

                def step(s, ph=ph):
                    g = dense_of(ph, s)
                    if ph == 1:
                        lagging(add_b1, s, 1, G)
                        lagging(lambda d: add_a0(1, d), s, -1, G)
                    if g:
                        dense_1(g)
                    if ph == 1:
                        lagging(lambda d: invert_degree(1, d), s, -1, G)
                    lagging(lambda d: equal(ph, d, seq(ph, d) - 1 - ph), s, -1, G)
                    if g:
                        dense_2(g)
                    if ph == 0:
                        lagging(lambda d: count_earlier(0, d), s, -1, G)
                    else:
                        lagging(lambda d: mean(1, d), s, -1, G)
                    if g:
                        dense_3(g)
                    if ph == 0:
                        lagging(lambda d: mask_rows(0, d), s, -1, G)
                    if g:
                        dense_4(g)
                    if ph == 0:
                        lagging(lambda d: add_spare(0, d), s, -1, G)
                        lagging(lambda d: write_rows(0, d), s, -1, G)

                steps(step, dve, R, G, ph * LAG1)
            for k in range(NG, NG + LAGD):
                dense_step(dense(k))

            equal(2, edge(0), 2 * G)
            all_kept(2)
            for f in (count_earlier, mask_rows, add_spare, write_rows, add_a0, invert_degree, mean):
                f(2, edge(0))

            def inverse_e(b):
                wait(dve, aSe, b.k + 1)
                v.reciprocal(rse[b.slot][:, :], sde[b.slot][:, :]).then_inc(dRse, 1)

            def normalise_e(b):
                wait(dve, dRse, b.k + 1)
                wait(dve, y_put[b.slot], 32 * b.lap)
                for c in range(2):
                    ins = v.tensor_scalar(ye[b.slot][:, c, :], re[:, c, :], mve[b.slot][:, c, 0:1], rse[b.slot][:, c:c + 1],
                                          ALU.subtract, ALU.mult)
                ins.then_inc(dNe, 1)

            def message(b):
                wait(dve, dNe, b.k + 1)
                wait(dve, ea_in[b.slot], 16 * (b.lap + 1) + (16 if b.is_any(G - 1) else 0))
                wait(dve, aV, G + b.k)
                v.tensor_tensor(pre[:, :, :], ye[b.slot][:, :, :], ea[b.slot][:, :, :], ALU.add).then_inc(dM, 1)

            def add_bout_e(b):
                wait(dve, dRe, b.k)
                v.tensor_tensor(xbe[:, :, :], kept_x(b),
                                bo_row[:, :].unsqueeze(1).broadcast_to([P, 2, D]), ALU.add).then_inc(dXe, 1)

            def residual_e(b):
                wait(dve, pYe, b.k + 1)
                wait(dve, dXe, b.k + 1)
                v.tensor_tensor(re[:, :, :], bY[:, 0:2 * D].rearrange("p (c d) -> p c d", c=2), xbe[:, :, :],
                                ALU.add).then_inc(dRe, 1)

            def statistics_e(b):
                wait(dve, dRe, b.k + 1)
                for c in range(2):
                    ins = v.bn_stats(ste[:, c, :], re[:, c, :])
                ins.then_inc(dSte, 1)

            def moments_e(b):
                wait(dve, dSte, b.k + 1)
                stand_alone(dve)
                for c in range(2):
                    ins = v.bn_aggr(mve[b.slot][:, c, :], ste[:, c, :])
                ins.then_inc(dMve, 1)

            def add_a1(s):
                wait(dve, pT2, s.k + 1)
                wait(dve, aS2, s.k)
                v.tensor_tensor(s1[:, :, :], bE2[:, 0:2 * D].rearrange("p (c d) -> p c d", c=2),
                                cs[s.slot][:, :, U:U + D], ALU.add).then_inc(dS1, 1)

            def step2(s):
                lagging(inverse_e, s, 3, G)
                lagging(add_a1, s, 1, G)
                lagging(normalise_e, s, 3, G)
                lagging(add_bout_e, s, 2, G)
                lagging(message, s, 3, G)
                lagging(lambda d: equal(2, d, 2 * G if isinstance(s.k, int) and s.k < 4 else 2 * G + d.k - 4), s, -1, G)
                lagging(residual_e, s, 2, G)
                lagging(lambda d: count_earlier(2, d), s, -1, G)
                lagging(statistics_e, s, 2, G)
                lagging(lambda d: mask_rows(2, d), s, -1, G)
                lagging(lambda d: add_a0(2, d), s, -1, G)
                lagging(moments_e, s, 2, G)
                lagging(lambda d: add_spare(2, d), s, -1, G)
                lagging(lambda d: invert_degree(2, d), s, -1, G)
                lagging(lambda d: write_rows(2, d), s, -1, G)
                lagging(lambda d: mean(2, d), s, -1, G)

            steps(step2, dve, R, G, LAG2)

            def sum3(g):
                p, j = dims(g)
                wait(dve, xt_in[g.slot], 16 * groups_in(g.slot) + 32 * (g.lap + 1))
                v.scalar_tensor_tensor(out=ta[g.slot][0:p, 0:j, :], in0=xt[g.slot][0:p, 0:j, :], scalar=eps1_col[0:p, 0:1],
                                       in1=ta[g.slot][0:p, 0:j, :], op0=ALU.mult, op1=ALU.add).then_inc(oH, 1)

            sum3(dense(0))
            sum3(dense(1))

            def step3(g):
                lagging(lambda b: residual(b, oM2, oB, True, oR), g, 1, NG)
                lagging(lambda b: inverse(b, oSd, oRs), g, 2, NG)
                lagging(lambda b: statistics(b, oR, oSt, oMv), g, 1, NG)
                lagging(lambda b: shift(b, oRs, oNm), g, 2, NG)
                lagging(sum3, g, -2, NG)
                lagging(lambda b: moments(b, oSt, oMv), g, 1, NG)

            steps(step3, dve, RD, NG, LAGD)

        @block.tensor
        def _(pe):
            mm = nc.tensor.matmul

            def transpose_x(g):
                p, j = dims(g)
                wait(pe, xt_in[g.slot], 16 * (g.lap + 1))
                wait(pe, aT, g.k)
                for q in range(j):
                    ins = nc.tensor.transpose(bT[:, q * p:(q + 1) * p], xt[g.slot][0:p, q, :], ident[0:p, 0:p])
                ins.then_inc(pT, 1)

            def product_1(g):
                p, j = dims(g)
                wait(pe, aT, g.k + 1)
                wait(pe, a1, g.k)
                mm(bH1[:, 0:p * j], w1_sb[:, :], xT[:, 0:p * j], start=True, stop=True).then_inc(p1, 1)

            def product_2(g):
                p, j = dims(g)
                wait(pe, a1, g.k + 1)
                wait(pe, a2, g.k)
                mm(bH2[:, 0:p * j], w2_sb[:, :], x1T[g.slot % 2][:, 0:p * j], start=True, stop=True).then_inc(p2, 1)

            def product_3(g):
                p, j = dims(g)
                wait(pe, a2, g.k + 1)
                wait(pe, dR, g.k)
                for q in range(j):
                    for h, t in enumerate((x1T[g.slot % 2], x2T)):
                        ins = mm(bY[0:p, q * D:(q + 1) * D], t[:, q * p:(q + 1) * p], wo_sb[:, h, :],
                                 start=(h == 0), stop=(h == 1))
                ins.then_inc(pY, 1)

            def dense_1(g):
                lagging(product_1, g, 0, NG)
                lagging(product_3, g, 1, NG)

            def dense_2(g):
                lagging(product_2, g, 0, NG)
                lagging(transpose_x, g, -1, NG)

            def dense_step(g):
                dense_1(g)
                dense_2(g)

            def sum_equal(s, width):
                for a in range(2):
                    for b in range(2):
                        ins = mm(bU[:, a * width:(a + 1) * width], S[s.slot][:, b, a * P:(a + 1) * P],
                                 V[s.slot][:, b, 0:width], start=(b == 0), stop=(b == 1))
                ins.then_inc(pU, 1)

            pe.wait_ge(pool_id, 2)
            pe.wait_ge(dve_c, 2)
            for n, b in enumerate((bE1, bE2)):
                ins = nc.tensor.transpose(b[:, 0:T], rows_f[n][:, :], ident[0:T, 0:T])
            ins.then_inc(rowsT, 1)
            pe.wait_ge(w_in, 16 * W_LOADS)
            transpose_x(dense(0))
            for k in range(PRE):
                dense_step(dense(k))

            def transpose_agg(ph, s):
                wait(pe, dAgg, seq(ph - 1, s) + 1)
                wait(pe, aTe, seq(ph - 1, s))
                for c in range(2):
                    ins = nc.tensor.transpose(bE1[:, c * P:(c + 1) * P], agg[s.slot][:, c, :], ident[:, :])
                ins.then_inc(pTe, 1)

            def product_1n(s):
                wait(pe, aTe, s.k + 1)
                wait(pe, dPre, s.k)
                for c in range(2):
                    ins = mm(bE2[:, c * D:(c + 1) * D], aggT[:, c * P:(c + 1) * P], w1_sb[:, :], start=True, stop=True)
                ins.then_inc(pXe, 1)

            def sums(ph, s):
                if ph == 0:
                    wait(pe, gathered[s.slot], 32 * (s.lap + 1))
                else:
                    wait(pe, aV, seq(ph - 1, s) + 1)
                wait(pe, dS, seq(ph, s) + 1)
                wait(pe, aU, seq(ph, s))
                sum_equal(s, D if ph == 2 else U)

            for ph in range(2):
                def step(s, ph=ph):
                    g = dense_of(ph, s)
                    if g:
                        dense_1(g)
                    if ph == 1:
                        lagging(lambda b: transpose_agg(1, b), s, 0, G)
                    if g:
                        dense_2(g)
                    if ph == 1:
                        lagging(product_1n, s, 0, G)
                    lagging(lambda b: sums(ph, b), s, ph * LAG1, G)

                if ph == 1:
                    for k in range(MID):
                        dense_step(dense(PRE + RD * R + k))
                steps(step, pe, R, G, ph * LAG1)
            for k in range(NG, NG + LAGD):
                dense_step(dense(k))

            def product_1e(s):
                wait(pe, aTe, G + s.k + 1)
                wait(pe, a1e, s.k)
                mm(bH1[:, 0:2 * P], w1_sb[:, :], aggT[:, :], start=True, stop=True).then_inc(p1e, 1)

            def transpose_x1(s):
                wait(pe, a1e, s.k + 1)
                wait(pe, dS1, s.k)
                if s.is_any(0):
                    pe.wait_ge(dPre, G)
                for c in range(2):
                    ins = nc.tensor.transpose(bE2[:, c * D:(c + 1) * D], x1Te[s.slot][:, c * P:(c + 1) * P], ident[:, :])
                ins.then_inc(pT2, 1)

            def transpose_s2(s):
                wait(pe, aS2, s.k + 1)
                wait(pe, aT3, s.k)
                for c in range(2):
                    ins = nc.tensor.transpose(bT[:, c * P:(c + 1) * P], s2[:, c, :], ident[:, :])
                ins.then_inc(pT3, 1)

            def product_2e(s):
                wait(pe, aT3, s.k + 1)
                wait(pe, a2e, s.k)
                mm(bH2[:, 0:2 * P], w2_sb[:, :], s2T[:, :], start=True, stop=True).then_inc(p2e, 1)

            def product_3e(b):
                wait(pe, a2e, b.k + 1)
                wait(pe, dRe, b.k)
                if b.is_any(0):
                    pe.wait_ge(dR, NG)
                for c in range(2):
                    for h, t in enumerate((x1Te[b.slot], x2Te)):
                        ins = mm(bY[:, c * D:(c + 1) * D], t[:, c * P:(c + 1) * P], wo_sb[:, h, :],
                                 start=(h == 0), stop=(h == 1))
                ins.then_inc(pYe, 1)

            def step2(s):
                lagging(transpose_x1, s, 1, G)
                lagging(lambda b: transpose_agg(2, b), s, 0, G)
                lagging(product_3e, s, 2, G)
                lagging(transpose_s2, s, 1, G)
                lagging(product_1e, s, 0, G)
                lagging(lambda b: sums(2, b), s, 3, G)
                lagging(product_2e, s, 1, G)

            steps(step2, pe, R, G, LAG2)

            def transpose_h(g):
                p, j = dims(g)
                wait(pe, oH, g.k + 1)
                wait(pe, oTc, g.k)
                for q in range(j):
                    ins = nc.tensor.transpose(bT[:, q * p:(q + 1) * p], ta[g.slot][0:p, q, :], ident[0:p, 0:p])
                ins.then_inc(oTp, 1)

            transpose_h(dense(0))

            def product_h1(g):
                p, j = dims(g)
                wait(pe, oTc, g.k + 1)
                wait(pe, oR1, g.k)
                mm(bH1[:, 0:p * j], v1_sb[:, :], xT[:, 0:p * j], start=True, stop=True).then_inc(oM1, 1)

            def product_h2(g):
                p, j = dims(g)
                wait(pe, oR1, g.k + 1)
                wait(pe, oR, g.k)
                if g.is_any(0):
                    pe.wait_ge(dRe, G)
                for q in range(j):
                    ins = mm(bY[0:p, q * D:(q + 1) * D], x1T[g.slot % 2][:, q * p:(q + 1) * p], v2_sb[:, :],
                             start=True, stop=True)
                ins.then_inc(oM2, 1)

            def step3(g):
                lagging(product_h1, g, 0, NG)
                lagging(transpose_h, g, -1, NG)
                lagging(product_h2, g, 1, NG)

            steps(step3, pe, RD, NG, LAGD)


_INS = ["x", "src", "dst", "edge_attr_128", "L0_gnn_W1", "L0_gnn_b1", "L0_gnn_W2", "L0_gnn_b2", "L0_gnn_Wout",
        "L0_gnn_bout", "L1_gnn_W1", "L1_gnn_b1", "L1_gnn_W2", "L1_gnn_b2", "L1_gnn_eps"]


def kernel(**inputs):
    import numpy as _np
    import concourse.bacc as _bacc
    from concourse import mybir as _mybir
    from concourse.bass_utils import run_bass_kernel_spmd as _run

    nc = _bacc.Bacc("TRN2", target_bir_lowering=False, num_devices=1)
    arrays, args = {}, []
    for name in _INS:
        a = _np.ascontiguousarray(inputs[name])
        if a.ndim == 0:
            a = a.reshape(1)
        arrays[f"in_{name}"] = a
        args.append(nc.dram_tensor(f"in_{name}", a.shape, _mybir.dt.from_np(a.dtype), kind="ExternalInput").ap())
    shape = inputs["x"].shape
    out = nc.dram_tensor("out_0", shape, _mybir.dt.float32, kind="ExternalOutput").ap()
    gnn(nc, *args, out)
    r = _run(nc, [arrays], core_ids=[0])
    return r.results[0]["out_0"]
```

```python
import concourse.bass as bass
from concourse import mybir
from contextlib import ExitStack

F32 = mybir.dt.float32
I32 = mybir.dt.int32
ALU = mybir.AluOpType
ACT = mybir.ActivationFunctionType

R = 7
RO = 6


class At:

    def __init__(self, ring, i, off):
        self.ring, self.i, self.off = ring, i, off
        self.k = ring * i + off
        self.slot = off % ring
        self.lap = i + off // ring

    def at(self, d):
        return At(self.ring, self.i, self.off + d)

    def is_any(self, *ks):
        return isinstance(self.k, int) and self.k in ks

    def is_from(self, k):
        return isinstance(self.k, int) and self.k >= k


def edge(k):
    return At(R, 0, k)


def dense(k):
    return At(R, 0, k)


def last(k):
    return At(RO, 0, k)


def steps(body, eng, ring, count, drain):
    laps = (count - 2 * ring) // ring
    for k in range(ring):
        body(At(ring, 0, k))
    with eng.Fori(0, laps) as i:
        for u in range(ring):
            body(At(ring, i, ring + u))
    for k in range(ring * (laps + 1), count + drain):
        body(At(ring, 0, k))


def lagging(stage, s, lag, count):
    if not (isinstance(s.k, int) and not 0 <= s.k - lag < count):
        stage(s.at(-lag))


def turn(g):
    return 2 if g.ring % 2 and g.slot == g.ring - 1 else g.slot % 2


def wait(eng, sem, value):
    if not (isinstance(value, int) and value == 0):
        eng.wait_ge(sem, value)


def gnn(nc, x, src, dst, edge_attr, w1, b1, w2, b2, wout, bout, v1, c1, v2, c2, eps, out):
    N, D = x.shape
    E = src.shape[0]
    P = 128
    T = -(-E // P)
    G = T // 2
    assert T == 2 * G and G == R * R
    ND = -(-N // (3 * P))
    FULL3 = ND - 1
    DLAST = N - FULL3 * 3 * P
    assert DLAST <= P and DLAST % 16 == 0
    NG = -(-N // (4 * P))
    assert NG == 2 * G
    FULL = NG - 1
    LEFT = N - FULL * 4 * P
    LP, LJ = LEFT // 3, 3
    assert LP * LJ == LEFT and LP % 16 == 0
    ELEFT = E - (T - 1) * P
    NT = -(-(N + 3 * P) // P) * P
    U = D + 4
    L = R - 1
    L2 = 4
    LAG1, LAG2, LAGD = 1, 3, 3
    MID = 2
    PRE = ND - 2 * G - 2 * MID
    PAIRS = -(-T // 4)
    PLEFT = T - 4 * (PAIRS - 1)
    FJ = 4 * NG
    EARLY = 4
    A0_CHUNKS, CHUNK = 28, FJ // G
    A0_CHUNK = FJ // A0_CHUNKS
    assert FJ == A0_CHUNK * A0_CHUNKS == CHUNK * G and A0_CHUNKS <= PRE + EARLY and N <= P * FJ <= NT and PAIRS < PRE
    LN_EPS = 1e-5

    C = nc.dram_tensor("sums_a0_a1", (NT, 2 * U), F32).ap()
    A2 = nc.dram_tensor("sums_a2", (NT, D), F32).ap()
    Y = nc.dram_tensor("table_y", (NT, D), F32).ap()
    XS = nc.dram_tensor("x_at_src", (P, T, D), F32).ap()
    SRCROWS = nc.dram_tensor("src_as_float", (T, P), F32).ap()
    DSTROWS = nc.dram_tensor("dst_as_float", (T, P), F32).ap()
    C_units = C.rearrange("n (s u) -> (n s) u", s=2)
    C_filled = C[0:P * FJ].rearrange("(p j) (s u) -> p j s u", p=P, s=2)
    C_rest = C[P * FJ:NT].rearrange("(j p) u -> p j u", p=P)
    A2_filled = A2[0:P * FJ].rearrange("(p j) d -> p j d", p=P)
    A2_rest = A2[P * FJ:NT].rearrange("(j p) d -> p j d", p=P)

    def groups(t, full, j):
        return t[0:full * j * P].rearrange("(g p j) d -> g p j d", p=P, j=j)

    def last_rows(t):
        return t[FULL * 4 * P:N].rearrange("(p j) d -> p j d", j=LJ)

    x3, y3 = groups(x, FULL3, 3), groups(Y, FULL3, 3)
    y4, a24, out4 = groups(Y, FULL, 4), groups(A2, FULL, 4), groups(out, FULL, 4)
    y_last, a2_last, out_last = last_rows(Y), last_rows(A2), last_rows(out)
    rb_src = SRCROWS.rearrange("(g c) p -> g (c p)", c=2)
    rb_dst = DSTROWS.rearrange("(g c) p -> g (c p)", c=2)
    ea2 = edge_attr[0:(T - 2) * P].rearrange("(g c p) d -> g p c d", c=2, p=P)

    ctx = ExitStack()
    with ctx:
        def sb(name, shape, dt=F32):
            return ctx.enter_context(nc.sbuf_tensor(name, shape, dt))

        def ring(name, shape, dt=F32, slots=R):
            return [sb(f"{name}{i}", shape, dt) for i in range(slots)]

        def bank(name):
            return ctx.enter_context(nc.psum_tensor(name, [P, 512], F32))

        def sem(name):
            return ctx.enter_context(nc.semaphore(name))

        def sems(name, slots=R):
            return [sem(f"{name}{i}") for i in range(slots)]

        ident = sb("ident", [P, P])
        eps1_ident = sb("eps1_ident", [P, P])
        zeros = sb("zeros", [P, 2 * U])
        earlier = sb("earlier", [P, 2, 2 * P])
        spare_i = sb("spare_i", [P, 2], I32)
        spare = sb("spare", [P, 2])
        w1_sb, w2_sb, v1_sb, v2_sb = (sb(n, [P, D]) for n in ("w1s", "w2s", "v1s", "v2s"))
        wo_sb = sb("wos", [P, 2, D])
        b1_col, b2_col, c1_col, eps_col, eps1_col, ln_col = (sb(n, [P, 1]) for n in ("b1c", "b2c", "c1c", "epc", "ep1", "lnc"))
        b1_row, bo_row, c2_row = (sb(n, [P, D]) for n in ("b1r", "bor", "c2r"))
        rows_i = [sb(f"rows_i{n}", [T, P], I32) for n in range(2)]
        rows_f = [sb(f"rows_f{n}", [T, P]) for n in range(2)]
        raw = [sb(f"raw{n}", [P, T]) for n in range(2)]
        off_spare = [sb(f"offs{n}", [P, G, 2]) for n in range(2)]
        near = [sb(f"near{n}", [P, T]) for n in range(2)]
        src_i, dst_i, unit_i = (sb(n, [P, T], I32) for n in ("src_i", "dst_i", "unit_i"))
        to_a1 = sb("to_a1", [P, T], I32)
        to_y = sb("to_y", [P, T], I32)
        V = ring("V", [P, 2, U])
        UU = ring("U", [P, 2, U])
        S = ring("S", [P, 2, 2 * P])
        rb = ring("rb", [P, 2 * P])
        cs = ring("cs", [P, 2, 2 * U])
        ea = ring("ea", [P, 2, D])
        ye = ring("ye", [P, 2, D])
        agg = ring("agg", [P, 2, D])
        xs = ring("xs", [P, 2, D])
        gi = ring("gi", [P, 2], I32)
        g4 = ring("g4", [P, 4], I32, slots=R)
        si = ring("si", [P, 2], I32)
        yi = ring("yi", [P, 2], I32)
        xkeep = sb("xkeep", [P, G, 2, D])
        aggT, s2T, x2Te = (sb(n, [P, 2 * P]) for n in ("aggT", "s2T", "x2Te"))
        x1Te = ring("x1Te", [P, 2 * P])
        pre, s1, s2, re, xbe = (sb(n, [P, 2, D]) for n in ("pre", "s1", "s2", "re", "xbe"))
        count, masked, row1 = (sb(n, [P, 2]) for n in ("count", "masked", "row1"))
        junk = sb("junk", [P, 2, 2 * P])
        deg, inv = (ring(n, [P, 2, 1]) for n in ("deg", "inv"))
        ste, mve = sb("ste", [P, 2, 6]), ring("mve", [P, 2, 2])
        sde, rse = (ring(n, [P, 2]) for n in ("sde", "rse"))
        xt = ring("xt", [P, 4, D])
        yd = ring("yd", [P, 4, D])
        four = [c[:, :, :].rearrange("p c u -> p (c u)")[:, 0:4 * D].rearrange("p (j d) -> p j d", j=4) for c in cs]
        xT, x2T = (sb(n, [P, 4 * P]) for n in ("xT", "x2T"))
        x1T = ring("x1T", [P, 4 * P], slots=3)
        st = sb("st", [P, 4, 6])
        mv = ring("mv", [P, 4, 2])
        sd, rs, nm = (ring(n, [P, 4]) for n in ("sd", "rs", "nm"))
        bT, bH1, bH2, bY, bE1, bE2, bU = (bank(n) for n in ("bT", "bH1", "bH2", "bY", "bE1", "bE2", "bU"))

        rb_in, gathered, added, y_put, ea_in = (sems(n) for n in ("rb_in", "gathered", "added", "y_put", "ea_in"))
        xt_in, y_out = (sems(n) for n in ("xt_in", "y_out"))
        xs_got, xs_moved = (sems(n) for n in ("xs_got", "xs_moved"))
        w_in, idx_in, rows_out, fill_a0, fill_a1, fill_a2 = (
            sem(n) for n in ("w_in", "idx_in", "rows_out", "fill_a0", "fill_a1", "fill_a2"))
        (pool_c, pool_id, spare_ok, rows_ok, dve_c, rowsT, idx_ok, gi_ok, g4_ok, eps1_ok, zeros_ok,
         v_ok, ln_ok) = (sem(n) for n in ("pool_c", "pool_id", "spare_ok", "rows_ok", "dve_c", "rowsT", "idx_ok",
                                          "gi_ok", "g4_ok", "eps1_ok", "zeros_ok", "v_ok", "ln_ok"))
        (pT, p1, p2, pY, aT, a1, a2, aS, aN, dX, dR, dSt, dMv, dRs, dNm) = (sem(n) for n in (
            "pT", "p1", "p2", "pY", "aT", "a1", "a2", "aS", "aN", "dX", "dR", "dSt", "dMv", "dRs", "dNm"))
        (dS, dCount, dMask, dRow, dSi, pU, aU, aKeep) = (sem(n) for n in (
            "dS", "dCount", "dMask", "dRow", "dSi", "pU", "aU", "aKeep"))
        (dDeg, dInv, dAgg, pTe, aTe, pXe, dPre, aV) = (sem(n) for n in (
            "dDeg", "dInv", "dAgg", "pTe", "aTe", "pXe", "dPre", "aV"))
        (p1e, a1e, pT2, dS1, aS2, pT3, aT3, p2e, a2e, pYe, dXe, dRe, dSte, dMve, aSe, dRse, dNe, dM) = (sem(n) for n in (
            "p1e", "a1e", "pT2", "dS1", "aS2", "pT3", "aT3", "p2e", "a2e", "pYe", "dXe", "dRe", "dSte", "dMve", "aSe",
            "dRse", "dNe", "dM"))
        (oH, oTp, oTc, oM1, oR1, oM2, oB, oR, oSt, oMv, oSd, oRs, oNm, oN, oNp) = (sem(n) for n in (
            "oH", "oTp", "oTc", "oM1", "oR1", "oM2", "oB", "oR", "oSt", "oMv", "oSd", "oRs", "oNm", "oN", "oNp"))

        waited = sem("waited")
        W_LOADS = 12
        block = ctx.enter_context(nc.Block())

        def dims(g):
            if g.ring == R:
                return (DLAST, 1) if g.is_any(ND - 1) else (P, 3)
            return (LP, LJ) if g.is_any(NG - 1) else (P, 4)

        def groups_in(slot):
            return len(range(slot, ND, R))

        def pairs_in(slot):
            return len(range(slot, PAIRS, R))

        def tiles_of(g):
            return PLEFT if g.is_any(PAIRS - 1) else 4

        def seq(ph, s):
            return G * ph + s.k

        def dense_of(ph, s):
            return None if s.is_from(G) else At(R, s.i, PRE + (G + MID) * ph + s.off)

        def after(ph):
            first = PRE + G + (G + MID) * ph
            return [dense(first + n) for n in range(MID + LAGD * ph)]

        def stand_alone(eng):
            eng.sem_inc(waited, 1)

        @block.sync
        def _(sp):
            sp.wait_ge(rows_ok, 2)
            for n, idx in enumerate((src, dst)):
                sp.dma_start(rows_i[n][0:T - 1, :], idx[0:(T - 1) * P].rearrange("(t p) -> t p", p=P)).then_inc(idx_in, 16)
                sp.dma_start(rows_i[n][T - 1:T, 0:ELEFT],
                             idx[(T - 1) * P:E].rearrange("(t p) -> t p", t=1)).then_inc(idx_in, 16)
            for dest, source in ((w1_sb[:, :], w1), (w2_sb[:, :], w2), (v1_sb[:, :], v1), (v2_sb[:, :], v2),
                                 (wo_sb[:, :, :], wout.rearrange("(h p) d -> p h d", h=2)),
                                 (b1_col[:, :], b1.rearrange("(p o) -> p o", o=1)),
                                 (b2_col[:, :], b2.rearrange("(p o) -> p o", o=1)),
                                 (c1_col[:, :], c1.rearrange("(p o) -> p o", o=1)),
                                 (b1_row[:, :], b1.partition_broadcast(P)),
                                 (bo_row[:, :], bout.partition_broadcast(P)),
                                 (c2_row[:, :], c2.partition_broadcast(P)),
                                 (eps_col[:, :], eps.partition_broadcast(P))):
                sp.dma_start(dest, source).then_inc(w_in, 16)

            def load_x(g):
                if g.is_any(ND - 1):
                    sp.dma_start(xt[g.slot][0:DLAST, 0, :], x[FULL3 * 3 * P:N]).then_inc(xt_in[g.slot], 16)
                else:
                    sp.dma_start(xt[g.slot][:, 0:3, :], x3[g.k]).then_inc(xt_in[g.slot], 16)

            def store_y(g):
                wait(sp, aN, g.k + 1)
                if g.is_any(ND - 1):
                    sp.dma_start(Y[FULL3 * 3 * P:N], yd[g.slot][0:DLAST, 0, :]).then_inc(y_out[g.slot], 16)
                else:
                    sp.dma_start(y3[g.k], yd[g.slot][:, 0:3, :]).then_inc(y_out[g.slot], 16)

            def next_x(g):
                wait(sp, dR, g.k - L)
                load_x(g)

            def dense_step(g):
                if not g.is_any(0):
                    lagging(next_x, g, 1 - L, ND)
                lagging(store_y, g, 3, ND)

            for k in range(2):
                load_x(dense(k))
            sp.wait_ge(zeros_ok, 1)
            sp.dma_start(C_rest, zeros[:, 0:2 * U].unsqueeze(1).broadcast_to([P, NT // P - FJ, 2 * U])).then_inc(fill_a0, 16)
            sp.wait_ge(dve_c, 2)
            sp.dma_start(SRCROWS, rows_f[0][:, :]).then_inc(rows_out, 16)
            sp.dma_start(DSTROWS, rows_f[1][:, :]).then_inc(rows_out, 16)

            def zeros_a0(g):
                sp.dma_start(C_filled[:, bass.ds(A0_CHUNK * g.k, A0_CHUNK), 0, :],
                             zeros[:, 0:U].unsqueeze(1).broadcast_to([P, A0_CHUNK, U])).then_inc(fill_a0, 16)

            for k in range(EARLY):
                zeros_a0(dense(k))
            for k in range(2, L):
                load_x(dense(k))
            def load_rb(ph, d):
                table = rb_dst if ph == 2 else rb_src
                sp.dma_start(rb[d.slot][:, :], table[d.k].partition_broadcast(P)).then_inc(rb_in[d.slot], 16)

            sp.wait_ge(rows_out, 32)
            for k in range(L):
                load_rb(0, edge(k))

            def put_xs(g):
                t = tiles_of(g)
                wait(sp, xs_got[g.slot], 64 * g.lap + 16 * t)
                sp.dma_start(XS[:, bass.ds(4 * g.k, t), :], four[g.slot][:, 0:t, :]).then_inc(xs_moved[g.slot], 16)

            def before(g):
                dense_step(g)
                lagging(zeros_a0, g, -EARLY, A0_CHUNKS)
                lagging(put_xs, g, 1, PAIRS)

            steps(before, sp, R, PRE, 0)
            sp.dma_start(A2_rest, zeros[:, 0:D].unsqueeze(1).broadcast_to([P, NT // P - FJ, D])).then_inc(fill_a2, 16)

            def zeros_a1(s):
                sp.dma_start(C_filled[:, bass.ds(CHUNK * s.k, CHUNK), 1, :],
                             zeros[:, 0:U].unsqueeze(1).broadcast_to([P, CHUNK, U])).then_inc(fill_a1, 16)

            def zeros_a2(s):
                sp.dma_start(A2_filled[:, bass.ds(CHUNK * s.k, CHUNK), :],
                             zeros[:, 0:D].unsqueeze(1).broadcast_to([P, CHUNK, D])).then_inc(fill_a2, 16)

            for ph in range(2):
                if ph == 1:
                    sp.wait_ge(dS, G)
                    for k in range(L):
                        load_rb(1, edge(k))

                def next_rb(d, ph=ph):
                    wait(sp, dS, seq(ph, d) - L)
                    load_rb(ph, d)

                def step(s, ph=ph):
                    lagging(next_rb, s, -L, G)
                    if g := dense_of(ph, s):
                        dense_step(g)
                    lagging((zeros_a1, zeros_a2)[ph], s, 0, G)

                if ph == 1:
                    for g in after(0):
                        dense_step(g)
                steps(step, sp, R, G, ph * LAG1)

            def load_ea(d):
                if d.is_any(G - 1):
                    sp.dma_start(ea[d.slot][:, 0, :], edge_attr[(T - 2) * P:(T - 1) * P]).then_inc(ea_in[d.slot], 16)
                    sp.dma_start(ea[d.slot][0:ELEFT, 1, :], edge_attr[(T - 1) * P:E]).then_inc(ea_in[d.slot], 16)
                else:
                    sp.dma_start(ea[d.slot][:, :, :], ea2[d.k]).then_inc(ea_in[d.slot], 16)

            sp.wait_ge(dS, 2 * G)
            for k in range(L):
                load_rb(2, edge(k))
            for k in range(LAG2):
                load_ea(edge(k))

            def load_xs(d):
                sp.dma_start(xs[d.slot][:, :, :], XS[:, bass.ds(2 * d.k, 2), :]).then_inc(xs_moved[d.slot], 16)

            for n in range(R):
                sp.wait_ge(xs_moved[n], 16 * pairs_in(n))
            for k in range(L2):
                load_xs(edge(k))
            for g in after(1):
                dense_step(g)

            def next_xs(d):
                if not d.is_any(*range(R)):
                    wait(sp, dXe, d.k - R + 1)
                load_xs(d)

            def next_rb(d):
                wait(sp, dS, seq(2, d) - L)
                load_rb(2, d)

            def next_ea(d):
                if not d.is_any(*range(R)):
                    wait(sp, dM, d.k - R + 1)
                load_ea(d)

            def step2(s):
                lagging(next_rb, s, -L, G)
                lagging(next_xs, s, -L2, G)
                lagging(next_ea, s, -LAG2, G)

            steps(step2, sp, R, G, LAG2)

            for n in range(R):
                sp.wait_ge(y_put[n], 32 * R)
                sp.wait_ge(added[n], 32 * 3 * R)

            def load_ya(g):
                if g.is_any(NG - 1):
                    sp.dma_start(xt[g.slot][0:LP, 0:LJ, :], y_last).then_inc(xt_in[g.slot], 16)
                    sp.dma_start(four[g.slot][0:LP, 0:LJ, :], a2_last).then_inc(xt_in[g.slot], 16)
                else:
                    sp.dma_start(xt[g.slot][:, :, :], y4[g.k]).then_inc(xt_in[g.slot], 16)
                    sp.dma_start(four[g.slot][:, :, :], a24[g.k]).then_inc(xt_in[g.slot], 16)

            def store_out(g):
                wait(sp, oN, g.k + 1)
                wait(sp, oNp, g.k + 1)
                if g.is_any(NG - 1):
                    sp.dma_start(out_last, yd[g.slot][0:LP, 0:LJ, :]).then_inc(y_out[g.slot], 16)
                else:
                    sp.dma_start(out4[g.k], yd[g.slot][:, :, :]).then_inc(y_out[g.slot], 16)

            for k in range(RO - 1):
                load_ya(last(k))

            def next_ya(g):
                wait(sp, oTp, g.k - RO + 1)
                wait(sp, oR, g.k - RO + 1)
                load_ya(g)

            def step3(g):
                if not g.is_any(0):
                    lagging(next_ya, g, 2 - RO, NG)
                lagging(store_out, g, 3, NG)

            steps(step3, sp, RO, NG, LAGD)
            for n in range(RO):
                sp.wait_ge(y_out[n], 16 * (groups_in(n) + len(range(n, NG, RO))))

        @block.gpsimd
        def _(pool):
            for n in range(2):
                nc.gpsimd.iota(rows_i[n][:, :], [[1, P]], base=N + 2 * P, channel_multiplier=0).then_inc(rows_ok, 1)
            nc.gpsimd.memset(ident[:, :], 0.0).then_inc(pool_c, 1)
            nc.gpsimd.memset(earlier[:, :, :], 1.0).then_inc(pool_c, 1)
            nc.gpsimd.iota(spare_i[:, :], [[P, 2]], base=N, channel_multiplier=1).then_inc(spare_ok, 1)
            pool.wait_ge(pool_c, 2)
            nc.gpsimd.affine_select(out=ident[:, :], in_=ident[:, :], compare_op=ALU.not_equal, fill=1.0, base=0,
                                    pattern=[[-1, P]], channel_multiplier=1).then_inc(pool_id, 1)
            nc.gpsimd.affine_select(out=earlier[:, :, :], in_=earlier[:, :, :], compare_op=ALU.is_gt, fill=0.0, base=0,
                                    pattern=[[P, 2], [-1, 2 * P]], channel_multiplier=1).then_inc(pool_id, 1)

            def rows_of(index, c):
                return bass.IndirectOffsetOnAxis(ap=index[:, c:c + 1], axis=0)

            def gather(ph, d):
                wait(pool, gi_ok, seq(ph, d) + 1)
                stand_alone(pool)
                for c in range(2):
                    if ph == 0:
                        pool.indirect_dma_start(out=V[d.slot][:, c, 0:D], out_offset=None, in_=x,
                                                in_offset=rows_of(gi[d.slot], c)).then_inc(gathered[d.slot], 16)
                    elif ph == 1:
                        pool.indirect_dma_start(out=cs[d.slot][:, c, 0:U], out_offset=None, in_=C_units,
                                                in_offset=rows_of(gi[d.slot], c)).then_inc(gathered[d.slot], 16)
                    else:
                        pool.indirect_dma_start(out=cs[d.slot][:, c, :], out_offset=None, in_=C,
                                                in_offset=rows_of(gi[d.slot], c)).then_inc(gathered[d.slot], 16)

            def add_rows(ph, s, index):
                wait(pool, aU, seq(ph, s) + 1)
                if not (ph == 0 and s.is_any(0)):
                    b = s.at(-1)
                    wait(pool, added[b.slot], 32 * (R * ph + b.lap + 1))
                stand_alone(pool)
                for c in range(2):
                    pool.indirect_dma_start(out=A2 if ph == 2 else C_units, out_offset=rows_of(index, c),
                                            in_=UU[s.slot][:, c, 0:D] if ph == 2 else UU[s.slot][:, c, :], in_offset=None,
                                            compute_op=ALU.add).then_inc(added[s.slot], 16)

            pool.wait_ge(idx_ok, 1)

            def copy_g4(g):
                wait(pool, xs_got[g.slot], 64 * g.lap)
                t = tiles_of(g)
                nc.gpsimd.tensor_copy(g4[g.slot][:, 0:t], src_i[:, bass.ds(4 * g.k, t)]).then_inc(g4_ok, 1)

            def gather_xs(g):
                wait(pool, g4_ok, g.k + 1)
                wait(pool, xs_moved[g.slot], 16 * g.lap)
                stand_alone(pool)
                for q in range(tiles_of(g)):
                    pool.indirect_dma_start(out=four[g.slot][:, q, :], out_offset=None, in_=x,
                                            in_offset=rows_of(g4[g.slot], q)).then_inc(xs_got[g.slot], 16)

            pool.wait_ge(v_ok, 1)
            for ph in range(2):
                if ph == 1:
                    pool.wait_ge(added[(G - 1) % R], 32 * R)
                if ph == 1:
                    for n in range(R):
                        pool.wait_ge(xs_moved[n], 16 * pairs_in(n))
                for k in range(L):
                    gather(ph, edge(k))
                if ph == 0:
                    copy_g4(dense(0))

                    def before(g):
                        lagging(copy_g4, g, -1, PAIRS)
                        gather_xs(g)

                    steps(before, pool, R, PAIRS, 0)
                    pool.wait_ge(fill_a0, 16 * (A0_CHUNKS + 1))
                else:
                    pool.wait_ge(fill_a1, 16 * G)

                def next_gather(d, ph=ph):
                    if ph == 0:
                        wait(pool, pU, d.k - L)
                        wait(pool, aKeep, d.k - L)
                    else:
                        wait(pool, dAgg, d.k - L)
                    gather(ph, d)

                def scatter(b, ph=ph):
                    wait(pool, dSi, seq(ph, b) + 1)
                    add_rows(ph, b, si[b.slot])

                def step(s, ph=ph):
                    lagging(next_gather, s, -L, G)
                    lagging(scatter, s, ph * LAG1, G)

                steps(step, pool, R, G, ph * LAG1)

            pool.wait_ge(added[(G - 1) % R], 32 * 2 * R)
            for k in range(L2):
                gather(2, edge(k))
            pool.wait_ge(fill_a2, 16 * (G + 1))
            for n in range(R):
                pool.wait_ge(y_out[n], 16 * groups_in(n))

            def put(b):
                wait(pool, dNe, b.k + 1)
                wait(pool, dSi, seq(2, b) + 1)
                if not b.is_any(0):
                    a = b.at(-1)
                    wait(pool, y_put[a.slot], 32 * (a.lap + 1))
                stand_alone(pool)
                for c in range(2):
                    pool.indirect_dma_start(out=Y, out_offset=rows_of(yi[b.slot], c), in_=ye[b.slot][:, c, :],
                                            in_offset=None).then_inc(y_put[b.slot], 16)
                add_rows(2, b, si[b.slot])

            def next_gather2(d):
                if not d.is_any(*range(R)):
                    wait(pool, dS1, d.k - R + 1)
                gather(2, d)

            def step2(s):
                lagging(next_gather2, s, -L2, G)
                lagging(put, s, LAG2, G)

            steps(step2, pool, R, G, LAG2)

            def scale_last(g):
                p, j = dims(g)
                wait(pool, oNm, g.k + 1)
                stand_alone(pool)
                nc.gpsimd.tensor_scalar(yd[g.slot][0:p, j - 1, :], yd[g.slot][0:p, j - 1, :], rs[g.slot][0:p, j - 1:j],
                                        nm[g.slot][0:p, j - 1:j], ALU.mult, ALU.add).then_inc(oNp, 1)

            def add_c2(g):
                p, j = dims(g)
                wait(pool, oTp, g.k + 1)
                nc.gpsimd.tensor_tensor(xt[g.slot][0:p, 0:j, :], xt[g.slot][0:p, 0:j, :],
                                        c2_row[0:p, :].unsqueeze(1).broadcast_to([p, j, D]), ALU.add).then_inc(oB, 1)

            def step3(g):
                lagging(add_c2, g, 0, NG)
                lagging(scale_last, g, 3, NG)

            steps(step3, pool, RO, NG, LAGD)

        @block.scalar
        def _(act):
            def copy_xT(g):
                p, j = dims(g)
                wait(act, pT, g.k + 1)
                wait(act, p1, g.k)
                nc.scalar.activation(xT[:, 0:p * j], bT[:, 0:p * j], ACT.Copy).then_inc(aT, 1)

            def root(g, moments, done):
                wait(act, moments, g.k + 1)
                p, j = dims(g)
                nc.scalar.activation(sd[g.slot][0:p, 0:j], mv[g.slot][0:p, 0:j, 1], ACT.Sqrt,
                                     bias=ln_col[0:p, :]).then_inc(done, 1)

            def scale(g, ready, done, others=0):
                p, j = dims(g)
                wait(act, ready, g.k + 1)
                for q in range(j - others):
                    ins = nc.scalar.activation(yd[g.slot][0:p, q, :], yd[g.slot][0:p, q, :], ACT.Identity,
                                               scale=rs[g.slot][0:p, q:q + 1], bias=nm[g.slot][0:p, q:q + 1])
                ins.then_inc(done, 1)

            def relu_1(g):
                p, j = dims(g)
                wait(act, p1, g.k + 1)
                if not g.is_any(0, 1):
                    wait(act, pY, g.k - 1)
                nc.scalar.activation(x1T[turn(g)][:, 0:p * j], bH1[:, 0:p * j], ACT.Relu, bias=b1_col[:, :]).then_inc(a1, 1)

            def relu_2(g):
                p, j = dims(g)
                wait(act, p2, g.k + 1)
                wait(act, pY, g.k)
                nc.scalar.activation(x2T[:, 0:p * j], bH2[:, 0:p * j], ACT.Relu, bias=b2_col[:, :]).then_inc(a2, 1)

            def dense_1(g):
                lagging(relu_1, g, 0, ND)

            def dense_2(g):
                lagging(relu_2, g, 0, ND)
                lagging(copy_xT, g, -1, ND)

            def dense_3(g):
                lagging(lambda b: root(b, dMv, aS), g, 2, ND)
                lagging(lambda b: scale(b, dNm, aN), g, 3, ND)

            def dense_step(g):
                dense_1(g)
                dense_3(g)
                dense_2(g)

            act.wait_ge(w_in, 16 * W_LOADS)
            act.wait_ge(ln_ok, 1)
            copy_xT(dense(0))
            steps(dense_step, act, R, PRE, 0)

            def keep_x(s):
                wait(act, gathered[s.slot], 32 * (s.lap + 1))
                nc.scalar.activation(xkeep[:, bass.ds(s.k, 1), :, :].rearrange("p a c d -> p (a c) d"),
                                     V[s.slot][:, :, 0:D], ACT.Copy).then_inc(aKeep, 1)

            def copy_aggT(ph, s):
                n = seq(ph - 1, s)
                wait(act, pTe, n + 1)
                if ph == 1:
                    wait(act, pXe, s.k)
                else:
                    wait(act, p1e, s.k)
                nc.scalar.activation(aggT[:, :], bE1[:, 0:2 * P], ACT.Copy).then_inc(aTe, 1)

            def relu_v(ph, s):
                wait(act, (None, dPre, dM)[ph], s.k + 1)
                nc.scalar.activation(V[s.slot][:, :, 0:D], pre[:, :, :], ACT.Relu).then_inc(aV, 1)

            def copy_sums(ph, s):
                wait(act, pU, seq(ph, s) + 1)
                wait(act, added[s.slot], 32 * (R * ph + s.lap))
                w = U if ph == 0 else D
                nc.scalar.activation(UU[s.slot][:, :, 0:w], bU[:, 0:2 * w].rearrange("p (c u) -> p c u", c=2),
                                     ACT.Copy).then_inc(aU, 1)

            for ph in range(2):
                def step(s, ph=ph):
                    g = dense_of(ph, s)
                    if g:
                        dense_1(g)
                    if ph == 0:
                        lagging(keep_x, s, 0, G)
                    else:
                        lagging(lambda b: relu_v(1, b), s, 1, G)
                        lagging(lambda b: copy_aggT(1, b), s, 0, G)
                    if g:
                        dense_3(g)
                        dense_2(g)
                    lagging(lambda b: copy_sums(ph, b), s, ph * LAG1, G)

                if ph == 1:
                    for g in after(0):
                        dense_step(g)
                steps(step, act, R, G, ph * LAG1)
            for g in after(1):
                dense_step(g)

            def relu_1e(s):
                wait(act, p1e, s.k + 1)
                if not s.is_any(*range(R)):
                    wait(act, pYe, s.k - R + 1)
                nc.scalar.activation(x1Te[s.slot][:, :], bH1[:, 0:2 * P], ACT.Relu, bias=b1_col[:, :]).then_inc(a1e, 1)

            def scale_s(s):
                wait(act, dS1, s.k + 1)
                wait(act, pT3, s.k)
                for c in range(2):
                    ins = nc.scalar.activation(s2[:, c, :], s1[:, c, :], ACT.Copy, scale=inv[s.slot][:, c, :])
                ins.then_inc(aS2, 1)

            def copy_s2T(s):
                wait(act, pT3, s.k + 1)
                wait(act, p2e, s.k)
                nc.scalar.activation(s2T[:, :], bT[:, 0:2 * P], ACT.Copy).then_inc(aT3, 1)

            def relu_2e(s):
                wait(act, p2e, s.k + 1)
                wait(act, pYe, s.k)
                nc.scalar.activation(x2Te[:, :], bH2[:, 0:2 * P], ACT.Relu, bias=b2_col[:, :]).then_inc(a2e, 1)

            def root_e(b):
                wait(act, dMve, b.k + 1)
                nc.scalar.activation(sde[b.slot][:, :], mve[b.slot][:, :, 1], ACT.Sqrt, bias=ln_col[:, :]).then_inc(aSe, 1)

            def step2(s):
                lagging(lambda b: copy_aggT(2, b), s, 0, G)
                lagging(scale_s, s, 1, G)
                lagging(lambda b: relu_v(2, b), s, 3, G)
                lagging(copy_s2T, s, 1, G)
                lagging(relu_1e, s, 0, G)
                lagging(lambda b: copy_sums(2, b), s, 3, G)
                lagging(relu_2e, s, 1, G)
                lagging(root_e, s, 2, G)

            steps(step2, act, R, G, LAG2)

            def copy_hT(g):
                p, j = dims(g)
                wait(act, oTp, g.k + 1)
                wait(act, oM1, g.k)
                nc.scalar.activation(xT[:, 0:p * j], bT[:, 0:p * j], ACT.Copy).then_inc(oTc, 1)

            copy_hT(last(0))

            def relu_3(g):
                p, j = dims(g)
                wait(act, oM1, g.k + 1)
                if not g.is_any(0, 1):
                    wait(act, oM2, g.k - 1)
                nc.scalar.activation(x1T[turn(g)][:, 0:p * j], bH1[:, 0:p * j], ACT.Relu, bias=c1_col[:, :]).then_inc(oR1, 1)

            def step3(g):
                lagging(relu_3, g, 0, NG)
                lagging(copy_hT, g, -1, NG)
                lagging(lambda b: root(b, oMv, oSd), g, 2, NG)
                lagging(lambda b: scale(b, oNm, oN, 1), g, 3, NG)

            steps(step3, act, RO, NG, LAGD)

        @block.vector
        def _(dve):
            v = nc.vector
            v.memset(zeros[:, :], 0.0).then_inc(zeros_ok, 1)
            v.memset(ln_col[:, :], LN_EPS).then_inc(ln_ok, 1)
            for n in range(R):
                ins = v.memset(V[n][:, :, D:U], 1.0)
            ins.then_inc(v_ok, 1)
            dve.wait_ge(idx_in, 64)
            for n in range(2):
                v.tensor_copy(rows_f[n][:, :], rows_i[n][:, :]).then_inc(dve_c, 1)
            dve.wait_ge(spare_ok, 1)
            v.tensor_copy(spare[:, :], spare_i[:, :]).then_inc(dve_c, 1)
            dve.wait_ge(rowsT, 1)
            for n, b in enumerate((bE1, bE2)):
                v.tensor_copy(raw[n][:, :], b[:, 0:T]).then_inc(dve_c, 1)
            dve.wait_ge(dve_c, 5)
            for n in range(2):
                v.tensor_scalar(near[n][:, :], raw[n][:, :], float(N - 1), None, ALU.min).then_inc(dve_c, 1)
                v.tensor_tensor(off_spare[n][:, :, :], raw[n][:, :].rearrange("p (g c) -> p g c", c=2),
                                spare[:, :].unsqueeze(1).broadcast_to([P, G, 2]), ALU.subtract).then_inc(dve_c, 1)
            dve.wait_ge(dve_c, 9)
            v.tensor_copy(src_i[:, :], near[0][:, :])
            v.tensor_scalar(unit_i[:, :], near[1][:, :], 2.0, None, ALU.mult)
            v.tensor_copy(dst_i[:, :], near[1][:, :]).then_inc(idx_ok, 1)

            def residual(g, product, other, stored, summed):
                p, j = dims(g)
                wait(dve, product, g.k + 1)
                wait(dve, other, g.k + 1)
                wait(dve, y_out[g.slot], 16 * ((groups_in(g.slot) if stored else 0) + g.lap))
                bank_y = (bY, bE1)[g.slot % 2] if stored else bY
                v.tensor_tensor(yd[g.slot][0:p, 0:j, :], bank_y[0:p, 0:j * D].rearrange("p (j d) -> p j d", j=j),
                                xt[g.slot][0:p, 0:j, :], ALU.add).then_inc(summed, 1)

            def statistics(g, summed, stats, done):
                p, j = dims(g)
                wait(dve, summed, g.k + 1)
                wait(dve, done, g.k)
                for q in range(j):
                    ins = v.bn_stats(st[0:p, q, :], yd[g.slot][0:p, q, :])
                ins.then_inc(stats, 1)

            def moments(g, stats, done):
                p, j = dims(g)
                wait(dve, stats, g.k + 1)
                stand_alone(dve)
                for q in range(j):
                    ins = v.bn_aggr(mv[g.slot][0:p, q, :], st[0:p, q, :])
                ins.then_inc(done, 1)

            def inverse(g, rooted, inverted):
                p, j = dims(g)
                wait(dve, rooted, g.k + 1)
                v.reciprocal(rs[g.slot][0:p, 0:j], sd[g.slot][0:p, 0:j]).then_inc(inverted, 1)

            def shift(g, inverted, done):
                p, j = dims(g)
                wait(dve, inverted, g.k + 1)
                v.scalar_tensor_tensor(out=nm[g.slot][0:p, 0:j], in0=mv[g.slot][0:p, 0:j, 0], scalar=-1.0,
                                       in1=rs[g.slot][0:p, 0:j], op0=ALU.mult, op1=ALU.mult).then_inc(done, 1)

            def add_bout(g):
                p, j = dims(g)
                wait(dve, pT, g.k + 1)
                v.tensor_tensor(xt[g.slot][0:p, 0:j, :], xt[g.slot][0:p, 0:j, :],
                                bo_row[0:p, :].unsqueeze(1).broadcast_to([p, j, D]), ALU.add).then_inc(dX, 1)

            def dense_1(g):
                lagging(add_bout, g, 0, ND)

            def dense_2(g):
                lagging(lambda b: residual(b, pY, dX, False, dR), g, 1, ND)

            def dense_3(g):
                lagging(lambda b: inverse(b, aS, dRs), g, 2, ND)
                lagging(lambda b: statistics(b, dR, dSt, dMv), g, 1, ND)

            def dense_4(g):
                lagging(lambda b: shift(b, dRs, dNm), g, 2, ND)
                lagging(lambda b: moments(b, dSt, dMv), g, 1, ND)

            def dense_step(g):
                dense_1(g)
                dense_2(g)
                dense_3(g)
                dense_4(g)

            def equal(ph, d, presums):
                which = 1 if ph == 2 else 0
                wait(dve, rb_in[d.slot], 16 * (R * ph + d.lap + 1))
                wait(dve, pU, presums)
                for c in range(2):
                    ins = v.tensor_scalar(S[d.slot][:, c, :], rb[d.slot][:, :], raw[which][:, bass.ds(2 * d.k + c, 1)], None,
                                          ALU.is_equal)
                ins.then_inc(dS, 1)

            def nth(ph, d):
                return (G if ph == 2 else 0) + d.k + 1

            def count_earlier(ph, d):
                wait(dve, dS, G * ph + d.k + 1)
                wait(dve, dSi, seq(ph, d))
                for c in range(2):
                    ins = v.tensor_tensor_reduce(out=junk[:, c, :], in0=S[d.slot][:, c, :], in1=earlier[:, c, :], scale=1.0,
                                                 scalar=0.0, op0=ALU.mult, op1=ALU.add, accum_out=count[:, c:c + 1])
                ins.then_inc(dCount, 1)

            def mask_rows(ph, d):
                which = 1 if ph == 2 else 0
                wait(dve, dCount, nth(ph, d))
                v.scalar_tensor_tensor(out=masked[:, :], in0=count[:, :], scalar=0.0,
                                       in1=off_spare[which][:, bass.ds(d.k, 1), :].rearrange("p a c -> p (a c)"),
                                       op0=ALU.is_equal, op1=ALU.mult).then_inc(dMask, 1)

            def add_spare(ph, d):
                wait(dve, dMask, nth(ph, d))
                v.tensor_tensor(row1[:, :], masked[:, :], spare[:, :], ALU.add).then_inc(dRow, 1)

            def rows_to(index, table, d):
                return v.tensor_copy(index[d.slot][:, :], table[:, bass.ds(2 * d.k, 2)])

            def gather_rows(ph, d):
                wait(dve, gathered[d.slot], 32 * (R * ph + d.lap))
                rows_to(gi, (dst_i, unit_i, src_i)[ph], d).then_inc(gi_ok, 1)

            def write_rows(ph, d):
                wait(dve, added[d.slot], 32 * (R * ph + d.lap))
                if ph == 1:
                    rows_to(si, to_a1, d).then_inc(dSi, 1)
                    return
                wait(dve, dRow, nth(ph, d))
                if ph == 2:
                    wait(dve, y_put[d.slot], 32 * d.lap)
                    rows_to(yi, to_y, d)
                if ph == 0:
                    v.tensor_scalar(to_a1[:, bass.ds(2 * d.k, 2)], row1[:, :], 2.0, 1.0, ALU.mult, ALU.add)
                    v.tensor_copy(to_y[:, bass.ds(2 * d.k, 2)], row1[:, :])
                v.tensor_scalar(si[d.slot][:, :], row1[:, :], 2.0 if ph == 0 else 1.0, None, ALU.mult).then_inc(dSi, 1)

            def add_a0(ph, d):
                wait(dve, gathered[d.slot], 32 * (R * ph + d.lap + 1))
                if ph == 1:
                    own = xkeep[:, bass.ds(d.k, 1), :, :].rearrange("p a c d -> p (a c) d")
                else:
                    wait(dve, xs_moved[d.slot], 16 * (pairs_in(d.slot) + d.lap + 1))
                    own = xs[d.slot][:, :, :]
                v.tensor_tensor(agg[d.slot][:, :, :], own, cs[d.slot][:, :, 0:D], ALU.add)
                v.tensor_scalar(deg[d.slot][:, :, :], cs[d.slot][:, :, D:D + 1], 1.0, 1.0, ALU.add, ALU.max).then_inc(dDeg, 1)

            def invert_degree(ph, d):
                wait(dve, dDeg, seq(ph - 1, d) + 1)
                v.reciprocal(inv[d.slot][:, :, :], deg[d.slot][:, :, :]).then_inc(dInv, 1)

            def mean(ph, d):
                wait(dve, dInv, seq(ph - 1, d) + 1)
                v.tensor_tensor(agg[d.slot][:, :, :], agg[d.slot][:, :, :], inv[d.slot][:, :, :].broadcast_to([P, 2, D]),
                                ALU.mult).then_inc(dAgg, 1)

            def add_b1(s):
                wait(dve, pXe, s.k + 1)
                wait(dve, aV, s.k)
                v.tensor_tensor(pre[:, :, :], bE2[:, 0:2 * D].rearrange("p (c d) -> p c d", c=2),
                                b1_row[:, :].unsqueeze(1).broadcast_to([P, 2, D]), ALU.add).then_inc(dPre, 1)

            dve.wait_ge(idx_ok, 1)
            for k in range(R):
                gather_rows(0, edge(k))
            dve.wait_ge(w_in, 16 * W_LOADS)
            v.tensor_scalar(eps1_col[:, :], eps_col[:, :], 1.0, None, ALU.add).then_inc(eps1_ok, 1)
            dve.wait_ge(eps1_ok, 1)
            dve.wait_ge(pool_id, 2)
            v.tensor_scalar(eps1_ident[:, :], ident[:, :], eps1_col[:, 0:1], None, ALU.mult).then_inc(eps1_ok, 1)
            steps(dense_step, dve, R, PRE, 0)

            for ph in range(2):
                if ph == 1:
                    for k in range(R):
                        gather_rows(1, edge(k))
                presums = G * ph
                equal(ph, edge(0), presums)
                if ph == 0:
                    for f in (count_earlier, mask_rows, add_spare, write_rows):
                        f(0, edge(0))
                else:
                    for g in after(0):
                        dense_step(g)
                    dve.wait_ge(aKeep, G)
                    for f in (add_a0, invert_degree, mean, write_rows):
                        f(1, edge(0))

                def step(s, ph=ph):
                    g = dense_of(ph, s)
                    if ph == 1:
                        lagging(add_b1, s, 1, G)
                        lagging(lambda d: add_a0(1, d), s, -1, G)
                    if g:
                        dense_1(g)
                    if ph == 1:
                        lagging(lambda d: invert_degree(1, d), s, -1, G)
                    lagging(lambda d: equal(ph, d, seq(ph, d) - 1 - ph), s, -1, G)
                    if g:
                        dense_2(g)
                    if ph == 0:
                        lagging(lambda d: count_earlier(0, d), s, -1, G)
                    else:
                        lagging(lambda d: mean(1, d), s, -1, G)
                    if g:
                        dense_3(g)
                    if ph == 0:
                        lagging(lambda d: mask_rows(0, d), s, -1, G)
                    if g:
                        dense_4(g)
                    if ph == 0:
                        lagging(lambda d: add_spare(0, d), s, -1, G)
                    lagging(lambda d: gather_rows(ph, d), s, -R, G)
                    lagging(lambda d: write_rows(ph, d), s, -1, G)

                steps(step, dve, R, G, ph * LAG1)

            for k in range(R):
                gather_rows(2, edge(k))
            equal(2, edge(0), 2 * G)
            for f in (count_earlier, mask_rows, add_spare, write_rows):
                f(2, edge(0))
            for g in after(1):
                dense_step(g)
            for f in (add_a0, invert_degree, mean):
                f(2, edge(0))

            def inverse_e(b):
                wait(dve, aSe, b.k + 1)
                v.reciprocal(rse[b.slot][:, :], sde[b.slot][:, :]).then_inc(dRse, 1)

            def normalise_e(b):
                wait(dve, dRse, b.k + 1)
                wait(dve, y_put[b.slot], 32 * b.lap)
                for c in range(2):
                    ins = v.tensor_scalar(ye[b.slot][:, c, :], re[:, c, :], mve[b.slot][:, c, 0:1], rse[b.slot][:, c:c + 1],
                                          ALU.subtract, ALU.mult)
                ins.then_inc(dNe, 1)

            def message(b):
                wait(dve, dNe, b.k + 1)
                wait(dve, ea_in[b.slot], 16 * (b.lap + 1) + (16 if b.is_any(G - 1) else 0))
                wait(dve, aV, G + b.k)
                v.tensor_tensor(pre[:, :, :], ye[b.slot][:, :, :], ea[b.slot][:, :, :], ALU.add).then_inc(dM, 1)

            def add_bout_e(b):
                wait(dve, dRe, b.k)
                v.tensor_tensor(xbe[:, :, :], xs[b.slot][:, :, :],
                                bo_row[:, :].unsqueeze(1).broadcast_to([P, 2, D]), ALU.add).then_inc(dXe, 1)

            def residual_e(b):
                wait(dve, pYe, b.k + 1)
                wait(dve, dXe, b.k + 1)
                v.tensor_tensor(re[:, :, :], bY[:, 0:2 * D].rearrange("p (c d) -> p c d", c=2), xbe[:, :, :],
                                ALU.add).then_inc(dRe, 1)

            def statistics_e(b):
                wait(dve, dRe, b.k + 1)
                for c in range(2):
                    ins = v.bn_stats(ste[:, c, :], re[:, c, :])
                ins.then_inc(dSte, 1)

            def moments_e(b):
                wait(dve, dSte, b.k + 1)
                stand_alone(dve)
                for c in range(2):
                    ins = v.bn_aggr(mve[b.slot][:, c, :], ste[:, c, :])
                ins.then_inc(dMve, 1)

            def add_a1(s):
                wait(dve, pT2, s.k + 1)
                wait(dve, aS2, s.k)
                v.tensor_tensor(s1[:, :, :], bE2[:, 0:2 * D].rearrange("p (c d) -> p c d", c=2),
                                cs[s.slot][:, :, U:U + D], ALU.add).then_inc(dS1, 1)

            def step2(s):
                lagging(inverse_e, s, 3, G)
                lagging(add_a1, s, 1, G)
                lagging(normalise_e, s, 3, G)
                lagging(add_bout_e, s, 2, G)
                lagging(message, s, 3, G)
                lagging(lambda d: equal(2, d, 2 * G if isinstance(s.k, int) and s.k < 4 else 2 * G + d.k - 4), s, -1, G)
                lagging(residual_e, s, 2, G)
                lagging(lambda d: count_earlier(2, d), s, -1, G)
                lagging(statistics_e, s, 2, G)
                lagging(lambda d: mask_rows(2, d), s, -1, G)
                lagging(lambda d: add_a0(2, d), s, -1, G)
                lagging(moments_e, s, 2, G)
                lagging(lambda d: add_spare(2, d), s, -1, G)
                lagging(lambda d: invert_degree(2, d), s, -1, G)
                lagging(lambda d: gather_rows(2, d), s, -R, G)
                lagging(lambda d: write_rows(2, d), s, -1, G)
                lagging(lambda d: mean(2, d), s, -1, G)

            steps(step2, dve, R, G, LAG2)

            def sum3(g):
                p, j = dims(g)
                j -= 1
                wait(dve, xt_in[g.slot], 16 * groups_in(g.slot) + 32 * (g.lap + 1))
                v.scalar_tensor_tensor(out=four[g.slot][0:p, 0:j, :], in0=xt[g.slot][0:p, 0:j, :], scalar=eps1_col[0:p, 0:1],
                                       in1=four[g.slot][0:p, 0:j, :], op0=ALU.mult, op1=ALU.add).then_inc(oH, 1)

            for k in range(2):
                sum3(last(k))

            def step3(g):
                lagging(sum3, g, -2, NG)
                lagging(lambda b: residual(b, oM2, oB, True, oR), g, 1, NG)
                lagging(lambda b: inverse(b, oSd, oRs), g, 2, NG)
                lagging(lambda b: statistics(b, oR, oSt, oMv), g, 1, NG)
                lagging(lambda b: shift(b, oRs, oNm), g, 2, NG)
                lagging(lambda b: moments(b, oSt, oMv), g, 1, NG)

            steps(step3, dve, RO, NG, LAGD)

        @block.tensor
        def _(pe):
            mm = nc.tensor.matmul

            def transpose_x(g):
                p, j = dims(g)
                wait(pe, xt_in[g.slot], 16 * (g.lap + 1))
                wait(pe, aT, g.k)
                for q in range(j):
                    ins = nc.tensor.transpose(bT[:, q * p:(q + 1) * p], xt[g.slot][0:p, q, :], ident[0:p, 0:p])
                ins.then_inc(pT, 1)

            def product_1(g):
                p, j = dims(g)
                wait(pe, aT, g.k + 1)
                wait(pe, a1, g.k)
                mm(bH1[:, 0:p * j], w1_sb[:, :], xT[:, 0:p * j], start=True, stop=True).then_inc(p1, 1)

            def product_2(g):
                p, j = dims(g)
                wait(pe, a1, g.k + 1)
                wait(pe, a2, g.k)
                mm(bH2[:, 0:p * j], w2_sb[:, :], x1T[turn(g)][:, 0:p * j], start=True, stop=True).then_inc(p2, 1)

            def product_3(g):
                p, j = dims(g)
                wait(pe, a2, g.k + 1)
                wait(pe, dR, g.k)
                for q in range(j):
                    for h, t in enumerate((x1T[turn(g)], x2T)):
                        ins = mm(bY[0:p, q * D:(q + 1) * D], t[:, q * p:(q + 1) * p], wo_sb[:, h, :],
                                 start=(h == 0), stop=(h == 1))
                ins.then_inc(pY, 1)

            def dense_1(g):
                lagging(product_1, g, 0, ND)

            def dense_2(g):
                lagging(product_3, g, 1, ND)
                lagging(product_2, g, 0, ND)
                lagging(transpose_x, g, -1, ND)

            def dense_step(g):
                dense_1(g)
                dense_2(g)

            def sum_equal(s, width):
                for a in range(2):
                    for b in range(2):
                        ins = mm(bU[:, a * width:(a + 1) * width], S[s.slot][:, b, a * P:(a + 1) * P],
                                 V[s.slot][:, b, 0:width], start=(b == 0), stop=(b == 1))
                ins.then_inc(pU, 1)

            pe.wait_ge(pool_id, 2)
            pe.wait_ge(dve_c, 2)
            for n, b in enumerate((bE1, bE2)):
                ins = nc.tensor.transpose(b[:, 0:T], rows_f[n][:, :], ident[0:T, 0:T])
            ins.then_inc(rowsT, 1)
            pe.wait_ge(w_in, 16 * W_LOADS)
            transpose_x(dense(0))
            steps(dense_step, pe, R, PRE, 0)

            def transpose_agg(ph, s):
                wait(pe, dAgg, seq(ph - 1, s) + 1)
                wait(pe, aTe, seq(ph - 1, s))
                for c in range(2):
                    ins = nc.tensor.transpose(bE1[:, c * P:(c + 1) * P], agg[s.slot][:, c, :], ident[:, :])
                ins.then_inc(pTe, 1)

            def product_1n(s):
                wait(pe, aTe, s.k + 1)
                wait(pe, dPre, s.k)
                for c in range(2):
                    ins = mm(bE2[:, c * D:(c + 1) * D], aggT[:, c * P:(c + 1) * P], w1_sb[:, :], start=True, stop=True)
                ins.then_inc(pXe, 1)

            def sums(ph, s):
                if ph == 0:
                    wait(pe, gathered[s.slot], 32 * (s.lap + 1))
                else:
                    wait(pe, aV, seq(ph - 1, s) + 1)
                wait(pe, dS, seq(ph, s) + 1)
                wait(pe, aU, seq(ph, s))
                sum_equal(s, U if ph == 0 else D)

            for ph in range(2):
                def step(s, ph=ph):
                    g = dense_of(ph, s)
                    if g:
                        dense_1(g)
                    if ph == 1:
                        lagging(lambda b: transpose_agg(1, b), s, 0, G)
                    if g:
                        dense_2(g)
                    if ph == 1:
                        lagging(product_1n, s, 0, G)
                    lagging(lambda b: sums(ph, b), s, ph * LAG1, G)

                if ph == 1:
                    for g in after(0):
                        dense_step(g)
                steps(step, pe, R, G, ph * LAG1)
            for g in after(1):
                dense_step(g)

            def product_1e(s):
                wait(pe, aTe, G + s.k + 1)
                wait(pe, a1e, s.k)
                mm(bH1[:, 0:2 * P], w1_sb[:, :], aggT[:, :], start=True, stop=True).then_inc(p1e, 1)

            def transpose_x1(s):
                wait(pe, a1e, s.k + 1)
                wait(pe, dS1, s.k)
                if s.is_any(0):
                    pe.wait_ge(dPre, G)
                for c in range(2):
                    ins = nc.tensor.transpose(bE2[:, c * D:(c + 1) * D], x1Te[s.slot][:, c * P:(c + 1) * P], ident[:, :])
                ins.then_inc(pT2, 1)

            def transpose_s2(s):
                wait(pe, aS2, s.k + 1)
                wait(pe, aT3, s.k)
                for c in range(2):
                    ins = nc.tensor.transpose(bT[:, c * P:(c + 1) * P], s2[:, c, :], ident[:, :])
                ins.then_inc(pT3, 1)

            def product_2e(s):
                wait(pe, aT3, s.k + 1)
                wait(pe, a2e, s.k)
                mm(bH2[:, 0:2 * P], w2_sb[:, :], s2T[:, :], start=True, stop=True).then_inc(p2e, 1)

            def product_3e(b):
                wait(pe, a2e, b.k + 1)
                wait(pe, dRe, b.k)
                if b.is_any(0):
                    pe.wait_ge(dR, ND)
                for c in range(2):
                    for h, t in enumerate((x1Te[b.slot], x2Te)):
                        ins = mm(bY[:, c * D:(c + 1) * D], t[:, c * P:(c + 1) * P], wo_sb[:, h, :],
                                 start=(h == 0), stop=(h == 1))
                ins.then_inc(pYe, 1)

            def step2(s):
                lagging(transpose_x1, s, 1, G)
                lagging(lambda b: transpose_agg(2, b), s, 0, G)
                lagging(product_3e, s, 2, G)
                lagging(transpose_s2, s, 1, G)
                lagging(product_1e, s, 0, G)
                lagging(lambda b: sums(2, b), s, 3, G)
                lagging(product_2e, s, 1, G)

            steps(step2, pe, R, G, LAG2)

            def transpose_h(g):
                p, j = dims(g)
                wait(pe, oH, g.k + 1)
                wait(pe, oTc, g.k)
                for q in range(j - 1):
                    nc.tensor.transpose(bT[:, q * p:(q + 1) * p], four[g.slot][0:p, q, :], ident[0:p, 0:p])
                q = j - 1
                mm(bT[:, q * p:(q + 1) * p], four[g.slot][0:p, q, :], ident[0:p, 0:p], start=True, stop=False)
                mm(bT[:, q * p:(q + 1) * p], xt[g.slot][0:p, q, :], eps1_ident[0:p, 0:p],
                   start=False, stop=True).then_inc(oTp, 1)

            pe.wait_ge(eps1_ok, 2)
            transpose_h(last(0))

            def product_h1(g):
                p, j = dims(g)
                wait(pe, oTc, g.k + 1)
                wait(pe, oR1, g.k)
                mm(bH1[:, 0:p * j], v1_sb[:, :], xT[:, 0:p * j], start=True, stop=True).then_inc(oM1, 1)

            def product_h2(g):
                p, j = dims(g)
                wait(pe, oR1, g.k + 1)
                if not g.is_any(0, 1):
                    wait(pe, oR, g.k - 1)
                if g.is_any(0):
                    pe.wait_ge(dRe, G)
                for q in range(j):
                    ins = mm((bY, bE1)[g.slot % 2][0:p, q * D:(q + 1) * D], x1T[turn(g)][:, q * p:(q + 1) * p], v2_sb[:, :],
                             start=True, stop=True)
                ins.then_inc(oM2, 1)

            def step3(g):
                lagging(product_h1, g, 0, NG)
                lagging(transpose_h, g, -1, NG)
                lagging(product_h2, g, 1, NG)

            steps(step3, pe, RO, NG, LAGD)


_INS = ["x", "src", "dst", "edge_attr_128", "L0_gnn_W1", "L0_gnn_b1", "L0_gnn_W2", "L0_gnn_b2", "L0_gnn_Wout",
        "L0_gnn_bout", "L1_gnn_W1", "L1_gnn_b1", "L1_gnn_W2", "L1_gnn_b2", "L1_gnn_eps"]


def kernel(**inputs):
    import numpy as _np
    import concourse.bacc as _bacc
    from concourse import mybir as _mybir
    from concourse.bass_utils import run_bass_kernel_spmd as _run

    nc = _bacc.Bacc("TRN2", target_bir_lowering=False, num_devices=1)
    arrays, args = {}, []
    for name in _INS:
        a = _np.ascontiguousarray(inputs[name])
        if a.ndim == 0:
            a = a.reshape(1)
        arrays[f"in_{name}"] = a
        args.append(nc.dram_tensor(f"in_{name}", a.shape, _mybir.dt.from_np(a.dtype), kind="ExternalInput").ap())
    shape = inputs["x"].shape
    out = nc.dram_tensor("out_0", shape, _mybir.dt.float32, kind="ExternalOutput").ap()
    gnn(nc, *args, out)
    r = _run(nc, [arrays], core_ids=[0])
    return r.results[0]["out_0"]
```
